# Optimizing a Trainium2 kernel written in Bass

```python
import numpy as np
import jax
import jax.numpy as jnp

def _softmax(x, axis=-1):
    return jax.nn.softmax(x, axis=axis)

def _gelu(x):
    return jax.nn.gelu(x, approximate=True)

def _silu(x):
    return jax.nn.silu(x)

def _sigmoid(x):
    return jax.nn.sigmoid(x)

def _layernorm(x, axis=-1, eps=1e-05):
    m = jnp.mean(x, axis=axis, keepdims=True)
    v = jnp.var(x, axis=axis, keepdims=True)
    return (x - m) / jnp.sqrt(v + eps)

def _scatter_add(tgt, idx, src, axis=0):
    return tgt.at[idx].add(src)

def _segment_sum(src, seg, n):
    return jax.ops.segment_sum(src, seg, n)
kernel_name = 'mk_seq_postln_d2_jaxref_r8_c25c16'

def setup_inputs(seed: int=0):
    np.random.seed(seed)
    _w = jnp.asarray

    def _L0_attn_setup():
        import jax, jax.numpy as jnp
        import numpy as np
        BS, N_CTX, WIDTH, HEADS = (4, 256, 128, 16)
        HEAD_DIM = WIDTH // HEADS
        key = jax.random.key(seed)
        k1, k2, k3 = jax.random.split(key, 3)
        init_scale = 0.02
        return {'x': jax.random.normal(k1, (BS, N_CTX, WIDTH), dtype=jnp.float32), 'Wqkv': jax.random.normal(k2, (WIDTH, 3 * WIDTH), dtype=jnp.float32) * init_scale, 'bqkv': jnp.zeros((3 * WIDTH,), dtype=jnp.float32), 'Wproj': jax.random.normal(k3, (WIDTH, WIDTH), dtype=jnp.float32) * init_scale, 'bproj': jnp.zeros((WIDTH,), dtype=jnp.float32)}
    _L0_attn_in = _L0_attn_setup()

    def _L0_ffn_setup():
        import jax, jax.numpy as jnp
        import numpy as np
        D_MODEL = 128
        EXPANSION = 4
        D_HIDDEN = D_MODEL * EXPANSION
        NUM_STAGES = int(np.log2(D_HIDDEN))

        def butterfly(y, weights, dim):
            lead = y.shape[:-1]
            for stage in range(weights.shape[0]):
                s = 2 ** stage
                nb = dim // (2 * s)
                yr = y.reshape(*lead, nb, 2, s)
                a = yr[..., 0, :]
                b = yr[..., 1, :]
                w = weights[stage].reshape(nb, s, 2, 2)
                na = w[..., 0, 0] * a + w[..., 0, 1] * b
                nb2 = w[..., 1, 0] * a + w[..., 1, 1] * b
                y = jnp.stack([na, nb2], axis=-2).reshape(*lead, dim)
            return y
        key = jax.random.key(seed)
        ks = jax.random.split(key, 6)
        B, S = (4, 256)
        x = jax.random.normal(ks[0], (B, S, D_MODEL), jnp.float32)
        W_exp = jax.random.normal(ks[1], (D_MODEL, D_HIDDEN), jnp.float32) * 0.02
        b_exp = jnp.zeros((D_HIDDEN,), jnp.float32)
        up_weights = jax.random.normal(ks[2], (NUM_STAGES, D_HIDDEN // 2, 2, 2), jnp.float32) * 0.02
        up_bias = jnp.zeros((D_HIDDEN,), jnp.float32)
        down_weights = jax.random.normal(ks[3], (NUM_STAGES, D_HIDDEN // 2, 2, 2), jnp.float32) * 0.02
        W_con = jax.random.normal(ks[4], (D_HIDDEN, D_MODEL), jnp.float32) * 0.02
        b_con = jnp.zeros((D_MODEL,), jnp.float32)
        down_bias = jnp.zeros((D_MODEL,), jnp.float32)
        return dict(x=x, W_exp=W_exp, b_exp=b_exp, up_weights=up_weights, up_bias=up_bias, down_weights=down_weights, W_con=W_con, b_con=b_con, down_bias=down_bias)
    _L0_ffn_in = _L0_ffn_setup()

    def _L1_attn_setup():
        import jax, jax.numpy as jnp
        import numpy as np
        B, S, E = (4, 256, 128)
        H, KVH = (16, 4)
        D = E // H
        QL, KVL = (64, 32)
        ROPE_BASE = 10000.0

        def _rope(x):
            d = x.shape[-1]
            inv_freq = 1.0 / ROPE_BASE ** (jnp.arange(0, d, 2, dtype=jnp.float32) / d)
            t = jnp.arange(x.shape[1], dtype=jnp.float32)
            freqs = jnp.outer(t, inv_freq)
            cos = jnp.cos(freqs)[None, :, None, :].astype(x.dtype)
            sin = jnp.sin(freqs)[None, :, None, :].astype(x.dtype)
            x1, x2 = (x[..., ::2], x[..., 1::2])
            r1 = x1 * cos - x2 * sin
            r2 = x1 * sin + x2 * cos
            return jnp.stack([r1, r2], axis=-1).reshape(x.shape)
        key = jax.random.key(seed)
        ks = jax.random.split(key, 7)
        s = 0.02
        return {'x': jax.random.normal(ks[0], (B, S, E), dtype=jnp.float32), 'Wqa': jax.random.normal(ks[1], (E, QL), dtype=jnp.float32) * s, 'Wqb': jax.random.normal(ks[2], (QL, E), dtype=jnp.float32) * s, 'Wkva': jax.random.normal(ks[3], (E, KVL), dtype=jnp.float32) * s, 'Wkvb': jax.random.normal(ks[4], (KVL, KVH * D * 2), dtype=jnp.float32) * s, 'Wout': jax.random.normal(ks[5], (E, E), dtype=jnp.float32) * s, 'bout': jax.random.normal(ks[6], (E,), dtype=jnp.float32) * s}
    _L1_attn_in = _L1_attn_setup()

    def _L1_ffn_setup():
        import jax, jax.numpy as jnp
        import numpy as np
        DIM = 128
        HIDDEN = 384
        SCALE = 1.0 / 127.0

        def _dequant(w_int, dtype):
            return w_int.astype(dtype) * jnp.asarray(SCALE, dtype)
        key = jax.random.key(seed)
        k_x, k_g, k_u, k_d = jax.random.split(key, 4)
        x = jax.random.normal(k_x, (4, 256, DIM), dtype=jnp.float32)
        w_gate = jax.random.randint(k_g, (HIDDEN, DIM), -127, 128, dtype=jnp.int32)
        w_up = jax.random.randint(k_u, (HIDDEN, DIM), -127, 128, dtype=jnp.int32)
        w_down = jax.random.randint(k_d, (DIM, HIDDEN), -127, 128, dtype=jnp.int32)
        return {'x': x, 'w_gate': w_gate, 'w_up': w_up, 'w_down': w_down}
    _L1_ffn_in = _L1_ffn_setup()
    _d = {'L0_attn_x': _L0_attn_in['x'], 'L0_attn_Wqkv': _L0_attn_in['Wqkv'], 'L0_attn_bqkv': _L0_attn_in['bqkv'], 'L0_attn_Wproj': _L0_attn_in['Wproj'], 'L0_attn_bproj': _L0_attn_in['bproj'], 'L0_ffn_W_exp': _L0_ffn_in['W_exp'], 'L0_ffn_b_exp': _L0_ffn_in['b_exp'], 'L0_ffn_up_weights': _L0_ffn_in['up_weights'], 'L0_ffn_up_bias': _L0_ffn_in['up_bias'], 'L0_ffn_down_weights': _L0_ffn_in['down_weights'], 'L0_ffn_W_con': _L0_ffn_in['W_con'], 'L0_ffn_b_con': _L0_ffn_in['b_con'], 'L0_ffn_down_bias': _L0_ffn_in['down_bias'], 'L1_attn_Wqa': _L1_attn_in['Wqa'], 'L1_attn_Wqb': _L1_attn_in['Wqb'], 'L1_attn_Wkva': _L1_attn_in['Wkva'], 'L1_attn_Wkvb': _L1_attn_in['Wkvb'], 'L1_attn_Wout': _L1_attn_in['Wout'], 'L1_attn_bout': _L1_attn_in['bout'], 'L1_ffn_w_gate': _L1_ffn_in['w_gate'], 'L1_ffn_w_up': _L1_ffn_in['w_up'], 'L1_ffn_w_down': _L1_ffn_in['w_down']}
    _x0 = _d['L0_attn_x']
    _d['L0_attn_x'] = jax.random.normal(jax.random.fold_in(jax.random.key(seed), 1), (8, 256, 128), dtype=_x0.dtype)
    del _x0
    return _d

def reference(L0_attn_x, L0_attn_Wqkv, L0_attn_bqkv, L0_attn_Wproj, L0_attn_bproj, L0_ffn_W_exp, L0_ffn_b_exp, L0_ffn_up_weights, L0_ffn_up_bias, L0_ffn_down_weights, L0_ffn_W_con, L0_ffn_b_con, L0_ffn_down_bias, L1_attn_Wqa, L1_attn_Wqb, L1_attn_Wkva, L1_attn_Wkvb, L1_attn_Wout, L1_attn_bout, L1_ffn_w_gate, L1_ffn_w_up, L1_ffn_w_down):

    def _L0_attn_ref(x, Wqkv, bqkv, Wproj, bproj):
        import jax, jax.numpy as jnp
        import numpy as np
        BS, N_CTX, WIDTH, HEADS = (4, 256, 128, 16)
        HEAD_DIM = WIDTH // HEADS
        bs, n_ctx, width = x.shape
        heads = HEADS
        d = width // heads
        qkv = x @ Wqkv + bqkv
        qkv = qkv.reshape(bs, n_ctx, heads, 3 * d)
        q, k, v = jnp.split(qkv, 3, axis=-1)
        scale = 1.0 / jnp.sqrt(jnp.asarray(d, dtype=x.dtype))
        scores = jnp.einsum('bqhd,bkhd->bhqk', q, k) * scale
        attn = jax.nn.softmax(scores, axis=-1)
        out = jnp.einsum('bhqk,bkhd->bqhd', attn, v)
        out = out.reshape(bs, n_ctx, width)
        return out @ Wproj + bproj

    def _L0_ffn_ref(x, W_exp, b_exp, up_weights, up_bias, down_weights, W_con, b_con, down_bias):
        import jax, jax.numpy as jnp
        import numpy as np
        D_MODEL = 128
        EXPANSION = 4
        D_HIDDEN = D_MODEL * EXPANSION
        NUM_STAGES = int(np.log2(D_HIDDEN))

        def butterfly(y, weights, dim):
            lead = y.shape[:-1]
            for stage in range(weights.shape[0]):
                s = 2 ** stage
                nb = dim // (2 * s)
                yr = y.reshape(*lead, nb, 2, s)
                a = yr[..., 0, :]
                b = yr[..., 1, :]
                w = weights[stage].reshape(nb, s, 2, 2)
                na = w[..., 0, 0] * a + w[..., 0, 1] * b
                nb2 = w[..., 1, 0] * a + w[..., 1, 1] * b
                y = jnp.stack([na, nb2], axis=-2).reshape(*lead, dim)
            return y
        h = jnp.einsum('bsd,dh->bsh', x, W_exp) + b_exp
        h = butterfly(h, up_weights, D_HIDDEN)
        h = jax.nn.gelu(h + up_bias, approximate=False)
        h = butterfly(h, down_weights, D_HIDDEN)
        y = jnp.einsum('bsh,hd->bsd', h, W_con) + b_con
        return y + down_bias

    def _L1_attn_ref(x, Wqa, Wqb, Wkva, Wkvb, Wout, bout):
        import jax, jax.numpy as jnp
        import numpy as np
        B, S, E = (4, 256, 128)
        H, KVH = (16, 4)
        D = E // H
        QL, KVL = (64, 32)
        ROPE_BASE = 10000.0

        def _rope(x):
            d = x.shape[-1]
            inv_freq = 1.0 / ROPE_BASE ** (jnp.arange(0, d, 2, dtype=jnp.float32) / d)
            t = jnp.arange(x.shape[1], dtype=jnp.float32)
            freqs = jnp.outer(t, inv_freq)
            cos = jnp.cos(freqs)[None, :, None, :].astype(x.dtype)
            sin = jnp.sin(freqs)[None, :, None, :].astype(x.dtype)
            x1, x2 = (x[..., ::2], x[..., 1::2])
            r1 = x1 * cos - x2 * sin
            r2 = x1 * sin + x2 * cos
            return jnp.stack([r1, r2], axis=-1).reshape(x.shape)
        b, s, _ = x.shape
        scale = D ** (-0.5)
        q = (x @ Wqa @ Wqb).reshape(b, s, H, D)
        kv = (x @ Wkva @ Wkvb).reshape(b, s, KVH, D, 2)
        k, v = (kv[..., 0], kv[..., 1])
        q = _rope(q)
        k = _rope(k)
        g = H // KVH
        k = jnp.repeat(k, g, axis=2)
        v = jnp.repeat(v, g, axis=2)
        scores = jnp.einsum('bqhd,bkhd->bhqk', q, k) * scale
        causal = jnp.triu(jnp.ones((s, s), dtype=bool), k=1)
        scores = jnp.where(causal[None, None], -jnp.inf, scores)
        w = jax.nn.softmax(scores, axis=-1)
        out = jnp.einsum('bhqk,bkhd->bqhd', w, v).reshape(b, s, E)
        return out @ Wout + bout

    def _L1_ffn_ref(x, w_gate, w_up, w_down):
        import jax, jax.numpy as jnp
        import numpy as np
        DIM = 128
        HIDDEN = 384
        SCALE = 1.0 / 127.0

        def _dequant(w_int, dtype):
            return w_int.astype(dtype) * jnp.asarray(SCALE, dtype)
        wg = _dequant(w_gate, x.dtype)
        wu = _dequant(w_up, x.dtype)
        wd = _dequant(w_down, x.dtype)
        gate = jnp.einsum('bsd,hd->bsh', x, wg)
        up = jnp.einsum('bsd,hd->bsh', x, wu)
        h = jax.nn.silu(gate) * up
        return jnp.einsum('bsh,dh->bsd', h, wd)
    x = L0_attn_x
    x = _layernorm(x + _L0_attn_ref(x, L0_attn_Wqkv, L0_attn_bqkv, L0_attn_Wproj, L0_attn_bproj), axis=-1)
    x = _layernorm(x + _L0_ffn_ref(x, L0_ffn_W_exp, L0_ffn_b_exp, L0_ffn_up_weights, L0_ffn_up_bias, L0_ffn_down_weights, L0_ffn_W_con, L0_ffn_b_con, L0_ffn_down_bias), axis=-1)
    x = _layernorm(x + _L1_attn_ref(x, L1_attn_Wqa, L1_attn_Wqb, L1_attn_Wkva, L1_attn_Wkvb, L1_attn_Wout, L1_attn_bout), axis=-1)
    x = _layernorm(x + _L1_ffn_ref(x, L1_ffn_w_gate, L1_ffn_w_up, L1_ffn_w_down), axis=-1)
    return x

_drawn_inputs = setup_inputs


def setup_inputs(seed=0):
    import zlib

    import numpy as np

    out = dict(_drawn_inputs(seed))
    spreads = {'L0_attn_bqkv': (0.0, 0.1),
     'L0_attn_bproj': (0.0, 0.1),
     'L0_ffn_b_exp': (0.0, 0.1),
     'L0_ffn_up_bias': (0.0, 0.1),
     'L0_ffn_b_con': (0.0, 0.1),
     'L0_ffn_down_bias': (0.0, 0.1)}
    factors = {'L0_attn_Wqkv': 8.0,
     'L1_attn_Wqa': 8.0,
     'L1_attn_Wqb': 8.0,
     'L1_attn_Wkva': 8.0,
     'L1_attn_Wkvb': 8.0,
     'L1_attn_Wout': 8.0,
     'L1_attn_bout': 4.212}
    for name, (base, spread) in spreads.items():
        noise = np.random.default_rng([zlib.crc32(name.encode()), seed]).standard_normal(out[name].shape)
        drawn = base * np.exp(spread * noise) if base else spread * noise
        out[name] = jnp.asarray(drawn.astype(out[name].dtype))
    for name, factor in factors.items():
        out[name] = (out[name] * factor).astype(out[name].dtype)
    return out
```

```python
import numpy as np
import concourse.bass as bass
from concourse import mybir
from contextlib import ExitStack

NB = 8
T = 256
W = 128
P = 128
H = 16
D = W // H
TOK = NB * T
NT = TOK // P
QT = T // P
HU = 512
HC = HU // P
STAGES = 9
INNER = 7
HS = 384
SC = HS // P
QLORA, KVLORA, KVH = 64, 32, 4
PARTS = 3
SROWS = PARTS * PARTS * D
MROW = 96
VP = 32
QH = 4
HEADS = NB * H
QUADS = HEADS // QH
FT = 512
NF = TOK // FT
FS = FT // P
EPS = 1e-5
SCALE = float(D) ** -0.5
MASKED = -1e30

LEAD = 24
AT_QK, AT_QK2, AT_V = -38, -37, -36
AT_MT = -7
PV_LAG = 6
MASK_LAG = 4
O_LAG = 11
AT_T, AT_ATT, AT_PROJ, AT_LN, AT_XT = 20, 23, 24, 25, 29
FIRST, LAST = AT_QK, H * (NB - 1) + AT_XT


def at_slot(g, offset, every=H, count=NB):
    n, rest = divmod(g - offset, every)
    return n if rest == 0 and 0 <= n < count else None


def block_kernel(nc, x_nat, x_t, wqk0, wv0, bqk0, bv0, wproj, bproj, u0, d0, bfw, bup, bcon, bdown,
                 perms, wqa_t, wqb, wkva_t, wkvb, wout, bout, rope_c, rope_s, wi_all, ident, causal, out):
    F32, BF, I32 = mybir.dt.float32, mybir.dt.bfloat16, mybir.dt.int32
    ALU = mybir.AluOpType
    ACT = mybir.ActivationFunctionType
    AX = mybir.AxisListType

    scratch = nc.dram_tensor("qk_parts", [2, NB, 2, PARTS, P, T], BF, kind="Internal").ap()

    ctx = ExitStack()
    with ctx:
        def sb(name, shape, dt=F32):
            return ctx.enter_context(nc.sbuf_tensor(name, shape, dt))

        def sem(name):
            return ctx.enter_context(nc.semaphore(name))

        wqk_sb = sb("wqk_sb", [P, 2, W])
        wv_sb = sb("wv_sb", [P, W])
        bqk_sb = sb("bqk_sb", [P, 2])
        bv_sb = sb("bv_sb", [P, W])
        wproj_sb = sb("wproj_sb", [P, W])
        bproj_sb = sb("bproj_sb", [P, W])
        up = [sb(f"up{i}", [P, HC, W + 1]) for i in range(2)]
        down = [sb(f"down{i}", [P, HC, W]) for i in range(2)]
        own = sb("own", [P, 2, HC, W + 1])
        bfw_sb = sb("bfw_sb", [P, 2, STAGES, 2, HC])
        bias4 = sb("bias4", [P, HC])
        perm_sb = sb("perm_sb", [P, INNER, P])
        bup_sb = sb("bup_sb", [P, HC])
        bhid = sb("bhid", [P, HC])
        bcon_sb = sb("bcon_sb", [P, W])
        bdown_sb = sb("bdown_sb", [P, W])
        wup = sb("wup", [P, HU])
        wqa_sb = sb("wqa_sb", [QLORA, W])
        wqb_sb = sb("wqb_sb", [QLORA, 2 * W])
        wkva_sb = sb("wkva_sb", [KVLORA, W])
        wkvb_sb = sb("wkvb_sb", [KVLORA, 3 * W])
        wl1 = sb("wl1", [P, 5, W])
        wout_sb = sb("wout_sb", [P, W])
        bout_sb = sb("bout_sb", [P, W])
        ropec_sb = sb("ropec_sb", [P, 2, T])
        ropes_sb = sb("ropes_sb", [P, 2, T])
        wi = sb("wi", [P, 3, HS], I32)
        wf = sb("wf", [P, 3, HS])
        id32 = sb("id32", [P, P])
        id16 = sb("id16", [P, P], BF)
        causal32 = sb("causal32", [P, T])
        causal_sb = sb("causal_sb", [P, T], BF)
        half = sb("half", [P, FS])
        xt = sb("xt", [P, TOK])
        xb = sb("xb", [P, NT, W])
        qk32 = sb("qk32", [P, 2, T])
        rope1 = sb("rope1", [P, 2, T])
        rope2 = sb("rope2", [P, 2, T])
        rest = sb("rest", [P, 2, T])
        parts = sb("parts", [P, 2, PARTS, 2, T], BF)
        Q = sb("Q", [P, 3, H, T], BF)
        K = sb("K", [P, 3, H, T], BF)
        V = sb("V", [P, 4, QT, H, VP])
        mx = sb("mx", [P, 2, QT, H])
        mrest = sb("mrest", [P, QT, H])
        mparts = sb("mparts", [P, QT, PARTS, H], BF)
        mt = sb("mt", [PARTS * H, 2, T], BF)
        E = sb("E", [P, 2, QH, 2 * T])
        O = sb("O", [P, 2, 2, 2, T])
        rec = sb("rec", [P, QT, H])
        at = sb("at", [P, QT, W])
        att = sb("att", [P, T])
        r = sb("r", [P, FS, W])
        stats = sb("stats", [P, FS, 6])
        mv = sb("mv", [P, FS, 2])
        ve = sb("ve", [P, FS])
        rstd = sb("rstd", [P, FS])
        ln = sb("ln", [P, 2, FS, W])
        hid = sb("hid", [P, 2, HC, FT])
        sg = sb("sg", [P, 2, FT])

        ST = [ctx.enter_context(nc.psum_tensor(f"ST{i}", [P, 2, 512], F32)) for i in range(2)]
        SM = [ctx.enter_context(nc.psum_tensor(f"SM{i}", [P, 512], F32)) for i in range(2)]
        PV = ctx.enter_context(nc.psum_tensor("PV", [P, 512], F32))
        MISC = ctx.enter_context(nc.psum_tensor("MISC", [P, 512], F32))

        ld = {n: sem(f"ld_{n}") for n in ("qk", "x", "v", "id", "perm", "bf", "xb", "proj", "l1", "next", "rope", "gate")}
        clean, v_clean = sem("clean"), sem("v_clean")
        id16_ready, causal_ready = sem("id16_ready"), sem("causal_ready")
        swap_ps, own_ready, stage_done = sem("swap_ps"), sem("own_ready"), sem("stage_done")
        wup_ps, wup_ready, bhid_ready = sem("wup_ps"), sem("wup_ready"), sem("bhid_ready")
        wl1_ps, wl1_ready, wf_ready = sem("wl1_ps"), sem("wl1_ready"), sem("wf_ready")
        xb0_ready, bnext_ready = sem("xb0_ready"), sem("bnext_ready")
        pool_chain, dve_chain = sem("pool_chain"), sem("dve_chain")
        AS = [{n: sem(f"a{l}_{n}") for n in (
            "qk_ps", "qk_out", "parts_ready", "wrote", "q_in", "k_in", "v_ps", "v_ready", "sm_ps", "max_done",
            "mparts_ready", "mt_ps", "mt_ready", "m_in", "st_ps", "exp_done", "masked", "pv_ps", "o_ready",
            "t_ps", "at_ready", "att_ps", "att_ready", "proj_ps", "res_done", "var_ready", "rstd_ready",
            "ln_ready", "xt_ps", "xt_ready", "xb_ready")} for l in range(2)]
        FF = [{n: sem(f"f{l}_{n}") for n in (
            "up_ps", "sg_ready", "hid_ready", "down_ps", "res_done", "var_ready", "rstd_ready", "ln_ready",
            "xt_ps", "xt_ready", "xb_ready")} for l in range(2)]
        stored = [sem(f"stored{i}") for i in range(2)]

        block = ctx.enter_context(nc.Block())

        def over_partitions(vec):
            return vec.rearrange("(a n) -> a n", a=1).broadcast_to([P, W])

        @block.sync
        def _(sp):
            sp.dma_start(xt[:, 0:T], x_t[:, 0:T]).then_inc(ld["x"], 16)
            sp.dma_start(wqk_sb[:, :, :], wqk0).then_inc(ld["qk"], 16)
            sp.dma_start(bqk_sb[:, :], bqk0).then_inc(ld["qk"], 16)
            sp.dma_start(wv_sb[:, :], wv0).then_inc(ld["v"], 16)
            sp.dma_start(bv_sb[:, :], over_partitions(bv0)).then_inc(ld["v"], 16)
            sp.dma_start(perm_sb[:, :, :], perms).then_inc(ld["perm"], 16)
            sp.dma_start(up[0][:, :, :], u0).then_inc(ld["bf"], 16)
            sp.dma_start(down[0][:, :, :], d0).then_inc(ld["bf"], 16)
            sp.dma_start(bfw_sb[:, :, :, :, :], bfw).then_inc(ld["bf"], 16)
            sp.dma_start(bup_sb[:, :], bup).then_inc(ld["bf"], 16)
            sp.dma_start(xt[:, T:TOK], x_t[:, T:TOK]).then_inc(ld["x"], 16)
            sp.dma_start(id32[:, :], ident).then_inc(ld["id"], 16)
            sp.dma_start(causal32[:, :], causal).then_inc(ld["id"], 16)

            def late_loads():
                sp.dma_start(xb[:, :, :], x_nat).then_inc(ld["xb"], 16)
                sp.dma_start(bproj_sb[:, :], over_partitions(bproj)).then_inc(ld["xb"], 16)
                for dst, src in ((wqa_sb, wqa_t), (wqb_sb, wqb), (wkva_sb, wkva_t), (wkvb_sb, wkvb)):
                    sp.dma_start(dst[:, :], src).then_inc(ld["l1"], 16)
                sp.dma_start(wproj_sb[:, :], wproj).then_inc(ld["proj"], 16)
                sp.dma_start(wout_sb[:, :], wout).then_inc(ld["next"], 16)
                for dst, src in ((bout_sb, bout), (bcon_sb, bcon), (bdown_sb, bdown)):
                    sp.dma_start(dst[:, :], over_partitions(src)).then_inc(ld["next"], 16)
                sp.dma_start(ropec_sb[:, :, :], rope_c).then_inc(ld["rope"], 16)
                sp.dma_start(ropes_sb[:, :, :], rope_s).then_inc(ld["rope"], 16)
                sp.dma_start(wi[:, :, :], wi_all).then_inc(ld["gate"], 16)

            def attention(l):
                S = AS[l]
                for g in range(FIRST, LAST + 1):
                    if (b := at_slot(g, AT_V)) is not None:
                        sp.wait_ge(S["parts_ready"], b + 1)
                        for s in range(2):
                            sp.dma_start(scratch[l, b, s].rearrange("a p t -> p a t"),
                                         parts[:, b % 2, :, s, :]).then_inc(S["wrote"], 16)
                        if l == 0 and b == 0:
                            sp.wait_ge(clean, 3)
                        sp.wait_ge(S["wrote"], 32 * (b + 1))
                        if b >= 3:
                            sp.wait_ge(S["st_ps"], H * (b - 2))
                        elif l == 1:
                            sp.wait_ge(AS[0]["st_ps"], HEADS)
                        for a in range(PARTS):
                            sp.dma_start(Q[PARTS * D * a:PARTS * D * (a + 1), b % 3, :, :],
                                         scratch[l, b, 0, a:a + 1].rearrange("a (d h) t -> a d (h t)", h=H)
                                         .broadcast_to([PARTS, D, H * T])).then_inc(S["q_in"], 16)
                        sp.dma_start(K[0:SROWS, b % 3, :, :],
                                     scratch[l, b, 1:2].rearrange("o a (d h) t -> o (a d) (h t)", h=H)
                                     .broadcast_to([PARTS, PARTS * D, H * T])).then_inc(S["k_in"], 16)
                        if l == 0 and b == 0:
                            late_loads()
                    if (b := at_slot(g, AT_MT)) is not None:
                        sp.wait_ge(S["mt_ready"], b + 1)
                        for a in range(PARTS):
                            sp.dma_start(Q[MROW + a:MROW + a + 1, b % 3, :, :],
                                         mt[H * a:H * (a + 1), b % 2, :]).then_inc(S["m_in"], 16)

            attention(0)
            attention(1)
            for n in range(NF):
                sp.wait_ge(FF[1]["ln_ready"], n + 1)
                sp.dma_start(out[:, n * FS:(n + 1) * FS, :], ln[:, n % 2, :, :]).then_inc(stored[n % 2], 16)
            for i in range(2):
                sp.wait_ge(stored[i], 16 * NF // 2)

        @block.tensor
        def _(pe):
            misc_read = []

            def misc(semaphore, value):
                if misc_read:
                    pe.wait_ge(*misc_read.pop())
                misc_read.append((semaphore, value))

            def butterfly(k):
                for c, (buf, s) in enumerate(((up, k), (down, STAGES - 1 - k))):
                    if s >= INNER:
                        continue
                    if k == 0:
                        pe.wait_ge(ld["bf"], 64)
                        pe.wait_ge(ld["perm"], 16)
                    else:
                        pe.wait_ge(stage_done, 2 * k)
                    src = buf[k % 2]
                    ins = nc.tensor.matmul(ST[c][:, 0, :], perm_sb[:, s, :], src[:, :, 0:W], start=True, stop=True)
                    if c == 0:
                        ins = nc.tensor.matmul(ST[c][:, 1, 0:HC], perm_sb[:, s, :], src[:, :, W], start=True, stop=True)
                    ins.then_inc(swap_ps, 1)

            def weights():
                pe.wait_ge(stage_done, 2 * STAGES)
                pe.wait_ge(ld["id"], 32)
                for c in range(HC):
                    ins = nc.tensor.transpose(ST[0][:, 0, c * P:(c + 1) * P], up[1][:, c, 0:W], id32[:, :])
                ins.then_inc(wup_ps, 1)
                pe.wait_ge(ld["l1"], 64)
                nc.tensor.matmul(ST[1][:, 0, 0:2 * W], wqa_sb[:, :], wqb_sb[:, :], start=True, stop=True)
                nc.tensor.matmul(ST[1][:, 1, 0:3 * W], wkva_sb[:, :], wkvb_sb[:, :], start=True, stop=True)\
                    .then_inc(wl1_ps, 1)

            def project(l, b, S, first, second):
                tokens = xt[:, b * T:(b + 1) * T]
                nc.tensor.matmul(MISC[:, 0:T], first, tokens, start=True, stop=True)
                nc.tensor.matmul(MISC[:, T:2 * T], second, tokens, start=True, stop=True).then_inc(S["qk_ps"], 1)

            def attention(l):
                S = AS[l]
                n_keys = (T, T) if l == 0 else (P, T)
                for g in range(FIRST, LAST + 1):
                    if (b := at_slot(g, AT_QK)) is not None:
                        misc(S["qk_out"], 2 * b + (2 if l == 0 else 1))
                        if l == 0:
                            if b <= 1:
                                pe.wait_ge(ld["x"], 16 * (b + 1))
                            if b == 0:
                                pe.wait_ge(ld["qk"], 32)
                            project(l, b, S, wqk_sb[:, 0, :], wqk_sb[:, 1, :])
                        else:
                            if b % 2 == 0:
                                pe.wait_ge(FF[0]["xt_ready"], b // 2 + 1)
                            project(l, b, S, wl1[:, 0, :], wl1[:, 2, :])
                    if l == 1 and (b := at_slot(g, AT_QK2)) is not None:
                        misc(S["qk_out"], 2 * b + 2)
                        project(l, b, S, wl1[:, 1, :], wl1[:, 3, :])
                    if (b := at_slot(g, AT_V)) is not None:
                        misc(S["v_ready"], b + 1)
                        if l == 0 and b == 0:
                            pe.wait_ge(ld["v"], 32)
                        for k in range(QT):
                            ins = nc.tensor.matmul(MISC[:, k * P:(k + 1) * P], xt[:, b * T + k * P:b * T + (k + 1) * P],
                                                   wv_sb[:, :] if l == 0 else wl1[:, 4, :], start=True, stop=True)
                        ins.then_inc(S["v_ps"], 1)
                    if l == 0 and (k := at_slot(g, -35, 2, STAGES)) is not None:
                        butterfly(k)
                    if l == 0 and g == -8:
                        weights()
                    m = g + LEAD
                    if 0 <= m < HEADS:
                        b, h = divmod(m, H)
                        if h == 0:
                            pe.wait_ge(S["q_in"], 48 * (b + 1))
                            pe.wait_ge(S["k_in"], 16 * (b + 1))
                        if m >= 2:
                            pe.wait_ge(S["max_done"], m - 1)
                        bank = SM[m % 2]
                        if l == 0:
                            for q in range(QT):
                                ins = nc.tensor.matmul(bank[:, q * T:(q + 1) * T], Q[0:MROW, b % 3, h, q * P:(q + 1) * P],
                                                       K[0:MROW, b % 3, h, :], start=True, stop=True)
                        else:
                            nc.tensor.matmul(bank[:, 0:T], Q[0:MROW, b % 3, h, P:T], K[0:MROW, b % 3, h, :],
                                             start=True, stop=False, skip_group_check=True)
                            nc.tensor.matmul(bank[:, T:T + P], Q[0:MROW, b % 3, h, 0:P], K[0:MROW, b % 3, h, 0:P],
                                             start=False, stop=False, skip_group_check=True)
                            if m == 0:
                                pe.wait_ge(causal_ready, 1)
                            ins = nc.tensor.matmul(bank[:, P:T + P], id16[:, :], causal_sb[:, :],
                                                   start=False, stop=True, skip_group_check=True)
                        ins.then_inc(S["sm_ps"], 1)
                    if (b := at_slot(g, AT_MT)) is not None:
                        misc(S["mt_ready"], b + 1)
                        if l == 0 and b == 0:
                            pe.wait_ge(id16_ready, 1)
                        pe.wait_ge(S["mparts_ready"], b + 1)
                        for q in range(QT):
                            ins = nc.tensor.transpose(MISC[:, :].bitcast(BF)[0:PARTS * H, q * P:(q + 1) * P],
                                                      mparts[:, q, :, :], id16[:, :])
                        ins.then_inc(S["mt_ps"], 1)
                    if 0 <= g < HEADS:
                        b, h = divmod(g, H)
                        if h == 0:
                            pe.wait_ge(S["m_in"], 48 * (b + 1))
                        if l == 0 and g == 0:
                            pe.wait_ge(wl1_ready, 2)
                            pe.wait_ge(wup_ready, 1)
                        if g >= 4 and g % 2 == 0:
                            pe.wait_ge(S["exp_done"], g // 2 - 1)
                        bank = ST[g // 2 % 2]
                        for k in range(QT):
                            q0 = k * P if l == 1 else 0
                            ins = nc.tensor.matmul(bank[:, g % 2, k * T:(k + 1) * T - q0], K[:, b % 3, h, k * P:(k + 1) * P],
                                                   Q[:, b % 3, h, q0:T], start=True, stop=True)
                        ins.then_inc(S["st_ps"], 1)
                    if (a := at_slot(g, PV_LAG, QH, QUADS)) is not None:
                        b, r4 = divmod(a, H // QH)
                        if l == 0:
                            pe.wait_ge(S["exp_done"], 2 * (a + 1))
                        else:
                            pe.wait_ge(S["masked"], 2 * (a + 1))
                        if r4 == 0:
                            pe.wait_ge(S["v_ready"], b + 1)
                        if a % 2 == 0 and a:
                            pe.wait_ge(S["o_ready"], a // 2)
                        for k in range(QT):
                            q0 = k * P if l == 1 else 0
                            for j in range(QH):
                                ins = nc.tensor.matmul(PV[VP * j:VP * (j + 1), a % 2 * T + q0:(a % 2 + 1) * T],
                                                       V[:, b % 4, k, QH * r4 + j, :], E[:, a % 2, j, k * T:(k + 1) * T - q0],
                                                       start=(k == 0), stop=(k == QT - 1))
                        ins.then_inc(S["pv_ps"], 1)
                    for q in range(QT):
                        if (b := at_slot(g, AT_T + q)) is not None:
                            misc(S["at_ready"], QT * b + q + 1)
                            pe.wait_ge(S["o_ready"], 2 * (b + 1))
                            if l == 0 and b == 0:
                                pe.wait_ge(ld["id"], 32)
                            for a in range(H // QH):
                                ins = nc.tensor.transpose(MISC[:, a * P:(a + 1) * P],
                                                          O[:, b % 2, a // 2, a % 2, q * P:(q + 1) * P], id32[:, :])
                            ins.then_inc(S["t_ps"], 1)
                    if (b := at_slot(g, AT_ATT)) is not None:
                        misc(S["att_ready"], b + 1)
                        pe.wait_ge(S["at_ready"], QT * (b + 1))
                        for q in range(QT):
                            ins = nc.tensor.transpose(MISC[:, q * P:(q + 1) * P], at[:, q, :], id32[:, :])
                        ins.then_inc(S["att_ps"], 1)
                    if (b := at_slot(g, AT_PROJ)) is not None:
                        misc(S["res_done"], b + 1)
                        pe.wait_ge(S["att_ready"], b + 1)
                        if b == 0:
                            pe.wait_ge(ld["proj" if l == 0 else "next"], 16 if l == 0 else 64)
                        for q in range(QT):
                            ins = nc.tensor.matmul(MISC[:, q * P:(q + 1) * P], att[:, q * P:(q + 1) * P],
                                                   (wproj_sb if l == 0 else wout_sb)[:, :], start=True, stop=True)
                        ins.then_inc(S["proj_ps"], 1)
                    if (b := at_slot(g, AT_XT)) is not None:
                        misc(S["xt_ready"], b + 1)
                        pe.wait_ge(S["ln_ready"], b + 1)
                        for q in range(QT):
                            ins = nc.tensor.transpose(MISC[:, q * P:(q + 1) * P], ln[:, b % 2, q, :], id32[:, :])
                        ins.then_inc(S["xt_ps"], 1)

            def ffn(l):
                F = FF[l]
                C = HC if l == 0 else SC

                def hidden(n):
                    if n == 0:
                        pe.wait_ge(AS[l]["exp_done"], HEADS // 2)
                        if l == 0:
                            pe.wait_ge(wup_ready, 1)
                        else:
                            pe.wait_ge(wf_ready, 1)
                    pe.wait_ge(AS[l]["xt_ready"], 2 * (n + 1))
                    tokens = xt[:, n * FT:(n + 1) * FT]
                    for c in range(C):
                        m = n * C + c
                        if l == 0:
                            if m >= HC:
                                pe.wait_ge(F["hid_ready"], m - HC + 1)
                            nc.tensor.matmul(ST[c // 2][:, c % 2, :], wup[:, c * P:(c + 1) * P], tokens,
                                             start=True, stop=True).then_inc(F["up_ps"], 1)
                        else:
                            if m >= 2:
                                pe.wait_ge(F["hid_ready"], m - 1)
                            for j in range(2):
                                nc.tensor.matmul(ST[j][:, m % 2, :], wf[:, j, c * P:(c + 1) * P], tokens,
                                                 start=True, stop=True).then_inc(F["up_ps"], 1)

                def back(n):
                    if n >= 2:
                        pe.wait_ge(F["res_done"], n - 1)
                    elif n == 0:
                        pe.wait_ge(AS[l]["max_done"], HEADS)
                        if l == 0:
                            pe.wait_ge(stage_done, 2 * STAGES)
                    pe.wait_ge(F["hid_ready"], C * (n + 1))
                    for s in range(FS):
                        for c in range(C):
                            w = down[1][:, c, :] if l == 0 else wf[:, 2, c * W:(c + 1) * W]
                            ins = nc.tensor.matmul(SM[n % 2][:, s * W:(s + 1) * W], hid[:, n % 2, c, s * P:(s + 1) * P], w,
                                                   start=(c == 0), stop=(c == C - 1))
                    ins.then_inc(F["down_ps"], 1)

                def turn(n):
                    if n == 0:
                        pe.wait_ge(AS[l]["o_ready"], QUADS // 2)
                    else:
                        pe.wait_ge(F["xt_ready"], n)
                    pe.wait_ge(F["ln_ready"], n + 1)
                    for s in range(FS):
                        ins = nc.tensor.transpose(PV[:, s * P:(s + 1) * P], ln[:, n % 2, s, :], id32[:, :])
                    ins.then_inc(F["xt_ps"], 1)

                hidden(0)
                for n in range(NF):
                    if n + 1 < NF:
                        hidden(n + 1)
                    back(n)
                    if l == 0 and n:
                        turn(n - 1)
                if l == 0:
                    turn(NF - 1)

            attention(0)
            ffn(0)
            pe.wait_ge(FF[0]["res_done"], NF)
            pe.wait_ge(FF[0]["xt_ready"], NF)
            pe.wait_ge(wl1_ready, 2)
            attention(1)
            ffn(1)

        @block.scalar
        def _(act):
            def attention(l):
                S = AS[l]
                for g in range(FIRST, LAST + 1):
                    if l == 0 and (b := at_slot(g, AT_QK)) is not None:
                        if b == 0:
                            act.wait_ge(ld["qk"], 32)
                        else:
                            act.wait_ge(S["parts_ready"], b)
                        act.wait_ge(S["qk_ps"], b + 1)
                        for s in range(2):
                            act.activation(qk32[:, s, :], MISC[:, s * T:(s + 1) * T], ACT.Identity,
                                           bias=bqk_sb[:, s:s + 1]).then_inc(S["qk_out"], 1)
                    if l == 0 and g == -7:
                        act.wait_ge(wup_ps, 1)
                        act.activation(wup[:, :], ST[0][:, 0, :], ACT.Copy).then_inc(wup_ready, 1)
                        act.wait_ge(wl1_ps, 1)
                        act.activation(wl1[:, 0:2, :], ST[1][:, 0, 0:2 * W], ACT.Copy).then_inc(wl1_ready, 1)
                        act.activation(wl1[:, 2:5, :], ST[1][:, 1, 0:3 * W], ACT.Copy).then_inc(wl1_ready, 1)
                    if (b := at_slot(g, AT_MT)) is not None:
                        act.wait_ge(S["mt_ps"], b + 1)
                        if b >= 2:
                            act.wait_ge(S["m_in"], 48 * (b - 1))
                        elif l == 1:
                            act.wait_ge(AS[0]["m_in"], 48 * NB)
                        act.activation(mt[:, b % 2, :], MISC[:, :].bitcast(BF)[0:PARTS * H, 0:T], ACT.Copy)\
                            .then_inc(S["mt_ready"], 1)
                    if (t := at_slot(g, 1, 2, HEADS // 2)) is not None:
                        a = t // 2
                        act.wait_ge(S["st_ps"], 2 * (t + 1))
                        if a >= 2:
                            act.wait_ge(S["pv_ps"], a - 1)
                        elif l == 1:
                            act.wait_ge(AS[0]["pv_ps"], QUADS)
                        n = 2 * T if l == 0 else T + P
                        j = t % 2 * 2
                        act.activation(E[:, a % 2, j:j + 2, 0:n], ST[t % 2][:, :, 0:n], ACT.Exp, scale=SCALE)\
                            .then_inc(S["exp_done"], 1)
                    if (n := at_slot(g, O_LAG, 2 * QH, QUADS // 2)) is not None:
                        b = n // 2
                        act.wait_ge(S["pv_ps"], 2 * (n + 1))
                        if b >= 2:
                            act.wait_ge(S["t_ps"], QT * (b - 1))
                        elif l == 1:
                            act.wait_ge(AS[0]["t_ps"], QT * NB)
                        act.activation(O[:, b % 2, n % 2, :, :], PV[:, :], ACT.Copy).then_inc(S["o_ready"], 1)
                    if (b := at_slot(g, AT_ATT)) is not None:
                        act.wait_ge(S["att_ps"], b + 1)
                        if b:
                            act.wait_ge(S["proj_ps"], b)
                        elif l == 1:
                            act.wait_ge(AS[0]["proj_ps"], NB)
                        act.activation(att[:, :], MISC[:, 0:T], ACT.Copy).then_inc(S["att_ready"], 1)
                    if (b := at_slot(g, AT_XT)) is not None:
                        act.wait_ge(S["xt_ps"], b + 1)
                        act.activation(xt[:, b * T:(b + 1) * T], MISC[:, 0:T], ACT.Copy).then_inc(S["xt_ready"], 1)

            def turned(n):
                act.wait_ge(FF[0]["xt_ps"], n + 1)
                act.activation(xt[:, n * FT:(n + 1) * FT], PV[:, :], ACT.Copy).then_inc(FF[0]["xt_ready"], 1)

            attention(0)
            act.wait_ge(bhid_ready, 1)
            for n in range(NF):
                if n >= 2:
                    act.wait_ge(FF[0]["down_ps"], n - 1)
                for c in range(HC):
                    act.wait_ge(FF[0]["up_ps"], n * HC + c + 1)
                    act.activation(hid[:, n % 2, c, :], ST[c // 2][:, c % 2, :], ACT.Gelu, bias=bhid[:, c:c + 1])\
                        .then_inc(FF[0]["hid_ready"], 1)
                if n >= 2:
                    turned(n - 2)
            turned(NF - 2)
            turned(NF - 1)
            attention(1)
            for m in range(NF * SC):
                act.wait_ge(FF[1]["up_ps"], 2 * m + 1)
                if m >= 2:
                    act.wait_ge(FF[1]["hid_ready"], m - 1)
                act.activation(sg[:, m % 2, :], ST[0][:, m % 2, :], ACT.Silu).then_inc(FF[1]["sg_ready"], 1)

        @block.vector
        def _(dve):
            links, swaps = [0], [0]

            def link(ins):
                links[0] += 1
                ins.then_inc(dve_chain, 1)
                dve.wait_ge(dve_chain, links[0])

            def butterfly(k):
                for c, (buf, s) in enumerate(((up, k), (down, STAGES - 1 - k))):
                    src, dst = buf[k % 2], buf[(k + 1) % 2]
                    w = bfw_sb[:, c, s, 1, :]
                    if k == 0 and c == 0:
                        dve.wait_ge(ld["bf"], 64)
                    elif k:
                        dve.wait_ge(stage_done, 2 * k)
                    if s < INNER:
                        swaps[0] += 1
                        dve.wait_ge(swap_ps, swaps[0])
                    dve.wait_ge(own_ready, 2 * k + c + 1)
                    for ch in range(HC):
                        if s < INNER:
                            partner = ST[c][:, 0, ch * P:(ch + 1) * P]
                        else:
                            partner = src[:, ch ^ (1 << (s - INNER)), 0:W]
                        ins = nc.vector.scalar_tensor_tensor(out=dst[:, ch, 0:W], in0=partner, scalar=w[:, ch:ch + 1],
                                                             in1=own[:, c, ch, 0:W], op0=ALU.mult, op1=ALU.add)
                    if c == 0:
                        if s < INNER:
                            link(nc.vector.tensor_tensor(bias4[:, :], ST[c][:, 1, 0:HC], w, ALU.mult))
                        else:
                            step = 1 << (s - INNER)
                            for ch in range(HC):
                                o = ch ^ step
                                ins = nc.vector.tensor_tensor(bias4[:, ch:ch + 1], src[:, o, W:W + 1], w[:, ch:ch + 1], ALU.mult)
                            link(ins)
                        ins = nc.vector.tensor_tensor(dst[:, :, W], bias4[:, :], own[:, c, :, W], ALU.add)
                    ins.then_inc(stage_done, 1)

            def statistics(n, var_ready):
                for s in range(n):
                    ins = nc.vector.bn_stats(stats[:, s, :], r[:, s, :])
                link(ins)
                for s in range(n):
                    ins = nc.vector.bn_aggr(mv[:, s, :], stats[:, s, :])
                link(ins)
                nc.vector.tensor_scalar(ve[:, 0:n], mv[:, 0:n, 1], EPS, None, ALU.add).then_inc(var_ready, 1)

            def normalise(n, parity, ln_ready):
                for s in range(n):
                    ins = nc.vector.tensor_scalar(ln[:, parity, s, :], r[:, s, :], mv[:, s, 0:1], rstd[:, s:s + 1],
                                                  ALU.subtract, ALU.mult)
                ins.then_inc(ln_ready, 1)

            def attention(l):
                S = AS[l]
                for g in range(FIRST, LAST + 1):
                    if l == 1:
                        for s, offset in enumerate((AT_QK, AT_QK2)):
                            if (b := at_slot(g, offset)) is not None:
                                if b == 0 and s == 0:
                                    dve.wait_ge(ld["rope"], 32)
                                if b:
                                    dve.wait_ge(S["parts_ready"], b)
                                dve.wait_ge(S["qk_ps"], 2 * b + s + 1)
                                nc.vector.tensor_tensor((rope1, rope2)[s][:, :, :], MISC[:, :].rearrange("p (s t) -> p s t", s=2),
                                                        (ropec_sb, ropes_sb)[s][:, :, :], ALU.mult).then_inc(S["qk_out"], 1)
                    if (b := at_slot(g, AT_V)) is not None:
                        dve.wait_ge(S["v_ps"], b + 1)
                        if l == 0 and b == 0:
                            dve.wait_ge(ld["v"], 32)
                            dve.wait_ge(v_clean, 2)
                        if b >= 4:
                            dve.wait_ge(S["pv_ps"], H // QH * (b - 3))
                        elif l == 1:
                            dve.wait_ge(AS[0]["pv_ps"], QUADS)
                        values = V[:, b % 4, :, :, 0:D]
                        found = MISC[:, 0:T].rearrange("p (k h d) -> p k h d", k=QT, h=H)
                        if l == 0:
                            for k in range(QT):
                                ins = nc.vector.tensor_tensor(values[:, k], found[:, k],
                                                              bv_sb[:, :].rearrange("p (h d) -> p h d", h=H), ALU.add)
                            ins.then_inc(S["v_ready"], 1)
                        else:
                            nc.vector.tensor_copy(values, found).then_inc(S["v_ready"], 1)
                    if l == 0 and g == -37:
                        dve.wait_ge(ld["id"], 32)
                        nc.vector.tensor_copy(id16[:, :], id32[:, :]).then_inc(id16_ready, 1)
                        nc.vector.tensor_copy(causal_sb[:, :], causal32[:, :]).then_inc(causal_ready, 1)
                    if l == 0 and (k := at_slot(g, -35, 2, STAGES)) is not None:
                        butterfly(k)
                    if l == 0 and g == -8:
                        dve.wait_ge(stage_done, 2 * STAGES)
                        nc.vector.tensor_tensor(bhid[:, :], up[1][:, :, W], bup_sb[:, :], ALU.add).then_inc(bhid_ready, 1)
                    m = g + LEAD
                    if 0 <= m < HEADS:
                        b, h = divmod(m, H)
                        dve.wait_ge(S["sm_ps"], m + 1)
                        bank = SM[m % 2]
                        if l == 0:
                            ins = nc.vector.tensor_reduce(mx[:, b % 2, :, h], bank[:, :].rearrange("p (q k) -> p q k", q=QT),
                                                          AX.X, ALU.max, negate=True)
                        else:
                            nc.vector.tensor_reduce(mx[:, b % 2, 1, h:h + 1], bank[:, 0:T], AX.X, ALU.max, negate=True)
                            ins = nc.vector.tensor_reduce(mx[:, b % 2, 0, h:h + 1], bank[:, T:T + P], AX.X, ALU.max, negate=True)
                        ins.then_inc(S["max_done"], 1)
                        if h == H - 1:
                            dve.wait_ge(S["max_done"], m + 1)
                            if b:
                                dve.wait_ge(S["mt_ps"], b)
                            elif l == 1:
                                dve.wait_ge(AS[0]["mt_ps"], NB)
                            link(nc.vector.tensor_copy(mparts[:, :, 0, :], mx[:, b % 2, :, :]))
                            link(nc.vector.tensor_tensor(mrest[:, :, :], mx[:, b % 2, :, :], mparts[:, :, 0, :], ALU.subtract))
                            link(nc.vector.tensor_copy(mparts[:, :, 1, :], mrest[:, :, :]))
                            nc.vector.tensor_tensor(mparts[:, :, 2, :], mrest[:, :, :], mparts[:, :, 1, :], ALU.subtract)\
                                .then_inc(S["mparts_ready"], 1)
                    for q in range(QT):
                        if (b := at_slot(g, AT_T + q)) is not None:
                            dve.wait_ge(S["t_ps"], QT * b + q + 1)
                            found = MISC[:, :].rearrange("p (h c) -> p h c", h=H)
                            link(nc.vector.reciprocal(rec[:, q, :], found[:, :, D]))
                            if b and q == 0:
                                dve.wait_ge(S["att_ps"], b)
                            elif l == 1 and b == 0:
                                dve.wait_ge(AS[0]["att_ps"], NB)
                            nc.vector.tensor_tensor(at[:, q, :].rearrange("p (h d) -> p h d", h=H), found[:, :, 0:D],
                                                    rec[:, q, :].unsqueeze(2).broadcast_to([P, H, D]), ALU.mult)\
                                .then_inc(S["at_ready"], 1)
                    if (b := at_slot(g, AT_PROJ)) is not None:
                        dve.wait_ge(S["proj_ps"], b + 1)
                        if l == 0 and b == 0:
                            dve.wait_ge(xb0_ready, 1)
                        if l == 1 and b % 2 == 0:
                            dve.wait_ge(FF[0]["xb_ready"], b // 2 + 1)
                        if b:
                            dve.wait_ge(S["ln_ready"], b)
                        elif l == 1:
                            dve.wait_ge(FF[0]["ln_ready"], NF)
                        nc.vector.tensor_tensor(r[:, 0:QT, :], MISC[:, 0:T].rearrange("p (q w) -> p q w", q=QT),
                                                xb[:, QT * b:QT * (b + 1), :], ALU.add).then_inc(S["res_done"], 1)
                        dve.wait_ge(S["res_done"], b + 1)
                        statistics(QT, S["var_ready"])
                    if (b := at_slot(g, AT_LN)) is not None:
                        dve.wait_ge(S["rstd_ready"], b + 1)
                        if b >= 2:
                            dve.wait_ge(S["xt_ps"], b - 1)
                            dve.wait_ge(S["xb_ready"], b - 1)
                        elif l == 1:
                            dve.wait_ge(FF[0]["xt_ps"], NF)
                            dve.wait_ge(FF[0]["xb_ready"], NF)
                        normalise(QT, b % 2, S["ln_ready"])

            def ffn(l):
                F = FF[l]

                def tail(n):
                    dve.wait_ge(F["down_ps"], n + 1)
                    dve.wait_ge(AS[l]["xb_ready"], 2 * (n + 1))
                    if n:
                        dve.wait_ge(F["ln_ready"], n)
                    else:
                        dve.wait_ge(AS[l]["ln_ready"], NB)
                    nc.vector.tensor_tensor(r[:, :, :], SM[n % 2][:, :].rearrange("p (q w) -> p q w", q=FS),
                                            xb[:, FS * n:FS * (n + 1), :], ALU.add).then_inc(F["res_done"], 1)
                    dve.wait_ge(F["res_done"], n + 1)
                    statistics(FS, F["var_ready"])
                    dve.wait_ge(F["rstd_ready"], n + 1)
                    if n < 2:
                        dve.wait_ge(AS[l]["xt_ps"], NB)
                        dve.wait_ge(AS[l]["xb_ready"], NB)
                    elif l == 0:
                        dve.wait_ge(F["xt_ps"], n - 1)
                        dve.wait_ge(F["xb_ready"], n - 1)
                    else:
                        dve.wait_ge(stored[n % 2], 16 * (n // 2))
                    normalise(FS, n % 2, F["ln_ready"])

                def gate(n):
                    if n >= 2:
                        dve.wait_ge(F["down_ps"], n - 1)
                    elif n == 0:
                        dve.wait_ge(FF[0]["down_ps"], NF)
                    for c in range(SC):
                        m = n * SC + c
                        dve.wait_ge(F["sg_ready"], m + 1)
                        dve.wait_ge(F["up_ps"], 2 * (m + 1))
                        nc.vector.tensor_tensor(hid[:, n % 2, c, :], ST[1][:, m % 2, :], sg[:, m % 2, :], ALU.mult)\
                            .then_inc(F["hid_ready"], 1)

                if l == 0:
                    for n in range(NF):
                        tail(n)
                else:
                    gate(0)
                    for n in range(NF):
                        if n + 1 < NF:
                            gate(n + 1)
                        tail(n)

            attention(0)
            ffn(0)
            attention(1)
            ffn(1)

        @block.gpsimd
        def _(pool):
            links = [0]

            def link(ins):
                links[0] += 1
                ins.then_inc(pool_chain, 1)
                pool.wait_ge(pool_chain, links[0])

            def split(b, S):
                if b >= 2:
                    pool.wait_ge(S["wrote"], 32 * (b - 1))
                p = parts[:, b % 2]
                link(nc.gpsimd.tensor_scalar(p[:, 0], qk32[:, :, :], 1.0, None, ALU.mult))
                link(nc.gpsimd.tensor_tensor(rest[:, :, :], qk32[:, :, :], p[:, 0], ALU.subtract))
                link(nc.gpsimd.tensor_scalar(p[:, 1], rest[:, :, :], 1.0, None, ALU.mult))
                nc.gpsimd.tensor_tensor(p[:, 2], rest[:, :, :], p[:, 1], ALU.subtract).then_inc(S["parts_ready"], 1)

            def butterfly(k):
                for c, (buf, s, n) in enumerate(((up, k, W + 1), (down, STAGES - 1 - k, W))):
                    if k == 0 and c == 0:
                        pool.wait_ge(ld["bf"], 64)
                    elif k:
                        pool.wait_ge(stage_done, 2 * (k - 1) + c + 1)
                    nc.gpsimd.tensor_tensor(own[:, c, :, 0:n], buf[k % 2][:, :, 0:n],
                                            bfw_sb[:, c, s, 0, :].unsqueeze(2).broadcast_to([P, HC, n]), ALU.mult)\
                        .then_inc(own_ready, 1)

            def attention(l):
                S = AS[l]
                for g in range(FIRST, LAST + 1):
                    if (b := at_slot(g, AT_V)) is not None:
                        pool.wait_ge(S["qk_out"], 2 * (b + 1))
                        if l == 1:
                            if b:
                                pool.wait_ge(S["parts_ready"], b)
                            link(nc.gpsimd.tensor_tensor(qk32[:, :, :], rope1[:, :, :], rope2[:, :, :], ALU.add))
                        split(b, S)
                        if l == 0 and b == 0:
                            clear()
                    if l == 0 and (k := at_slot(g, -35, 2, STAGES)) is not None:
                        butterfly(k)
                    if l == 0 and g == -4:
                        pool.wait_ge(ld["xb"], 32)
                        nc.gpsimd.tensor_tensor(xb[:, :, :], xb[:, :, :],
                                                bproj_sb[:, :].unsqueeze(1).broadcast_to([P, NT, W]), ALU.add)\
                            .then_inc(xb0_ready, 1)
                        pool.wait_ge(ld["next"], 64)
                        nc.gpsimd.tensor_tensor(bcon_sb[:, :], bcon_sb[:, :], bdown_sb[:, :], ALU.add)\
                            .then_inc(bnext_ready, 1)
                        pool.wait_ge(ld["gate"], 16)
                        nc.gpsimd.tensor_scalar(wf[:, :, :], wi[:, :, :], 1.0 / 127.0, None, ALU.mult).then_inc(wf_ready, 1)
                    if l == 1 and (a := at_slot(g, MASK_LAG, QH, QUADS)) is not None:
                        pool.wait_ge(S["exp_done"], 2 * (a + 1))
                        for c in (0, T):
                            e = E[:, a % 2, :, c:c + P]
                            nc.gpsimd.affine_select(out=e, in_=e, pattern=[[0, QH], [1, P]], compare_op=ALU.is_ge,
                                                    fill=0.0, base=0, channel_multiplier=-1).then_inc(S["masked"], 1)
                    if (b := at_slot(g, AT_PROJ)) is not None:
                        pool.wait_ge(S["var_ready"], b + 1)
                        nc.gpsimd.tensor_tensor(rstd[:, 0:QT], ve[:, 0:QT], half[:, 0:QT], ALU.pow).then_inc(S["rstd_ready"], 1)
                    if (b := at_slot(g, AT_LN)) is not None:
                        pool.wait_ge(S["ln_ready"], b + 1)
                        dst, src = xb[:, QT * b:QT * (b + 1), :], ln[:, b % 2, 0:QT, :]
                        if l == 0:
                            if b == 0:
                                pool.wait_ge(bnext_ready, 1)
                            nc.gpsimd.tensor_tensor(dst, src, bcon_sb[:, :].unsqueeze(1).broadcast_to([P, QT, W]), ALU.add)\
                                .then_inc(S["xb_ready"], 1)
                        else:
                            nc.gpsimd.tensor_scalar(dst, src, 1.0, None, ALU.mult).then_inc(S["xb_ready"], 1)

            def clear():
                nc.gpsimd.memset(V[:, :, :, :, :], 0.0).then_inc(v_clean, 1)
                pool.wait_ge(v_clean, 1)
                nc.gpsimd.memset(V[:, :, :, :, D:D + 1], 1.0).then_inc(v_clean, 1)
                pool.wait_ge(v_clean, 2)
                for x in (Q, K):
                    nc.gpsimd.memset(x[64:P, :, :, :].bitcast(F32), 0.0).then_inc(clean, 1)
                pool.wait_ge(clean, 2)
                nc.gpsimd.memset(K[MROW:MROW + PARTS, :, :, :], 1.0).then_inc(clean, 1)
                pool.wait_ge(clean, 3)

            link(nc.gpsimd.memset(half[:, :], -0.5))
            attention(0)
            for n in range(NF):
                pool.wait_ge(FF[0]["var_ready"], n + 1)
                nc.gpsimd.tensor_tensor(rstd[:, :], ve[:, :], half[:, :], ALU.pow).then_inc(FF[0]["rstd_ready"], 1)
                pool.wait_ge(FF[0]["ln_ready"], n + 1)
                nc.gpsimd.tensor_tensor(xb[:, FS * n:FS * (n + 1), :], ln[:, n % 2, :, :],
                                        bout_sb[:, :].unsqueeze(1).broadcast_to([P, FS, W]), ALU.add)\
                    .then_inc(FF[0]["xb_ready"], 1)
            attention(1)
            for n in range(NF):
                pool.wait_ge(FF[1]["var_ready"], n + 1)
                nc.gpsimd.tensor_tensor(rstd[:, :], ve[:, :], half[:, :], ALU.pow).then_inc(FF[1]["rstd_ready"], 1)


def _features():
    d, h = np.meshgrid(np.arange(D), np.arange(H), indexing="ij")
    return d.ravel(), h.ravel()


def _constants():
    d, _ = _features()
    inv = (1.0 / np.float32(10000.0) ** (np.arange(0, D, 2, dtype=np.float32) / np.float32(D))).astype(np.float32)
    freqs = np.outer(np.arange(T, dtype=np.float32), inv).astype(np.float32)
    c = np.cos(freqs).astype(np.float32).T[d // 2]
    s = np.sin(freqs).astype(np.float32).T[d // 2] * np.where(d % 2 == 0, -1.0, 1.0).astype(np.float32)[:, None]
    i = np.arange(P)
    perms = np.zeros((P, INNER, P), np.float32)
    for k in range(INNER):
        perms[i, k, i ^ (1 << k)] = 1.0
    later = np.where(i[None, :] > i[:, None], np.float32(MASKED), np.float32(0.0))
    return {
        "rope_c": np.stack([c, c], 1), "rope_s": np.stack([s, s], 1), "perms": perms,
        "ident": np.eye(P, dtype=np.float32), "causal": np.concatenate([later, later], 1).astype(np.float32),
    }


def _butterfly_layout(up_weights, down_weights):
    f = np.arange(HU)
    out = np.empty((HU, 2, STAGES, 2), np.float32)
    for s in range(STAGES):
        k, j = (f >> (s + 1) << s) + f % (1 << s), f >> s & 1
        out[:, 0, s, 0], out[:, 0, s, 1] = up_weights[s, k, j, j], up_weights[s, k, j, 1 - j]
        out[:, 1, s, 0], out[:, 1, s, 1] = down_weights[s, k, j, j], down_weights[s, k, 1 - j, j]
    return out.reshape(HC, P, 2, STAGES, 2).transpose(1, 2, 3, 4, 0)


def _arrays(a):
    d, h = _features()
    wqkv, bqkv = a["L0_attn_Wqkv"], a["L0_attn_bqkv"]
    x = a["L0_attn_x"].reshape(NT, P, W)
    heads, dims = np.arange(W) // D, np.arange(W) % D
    cols = [3 * D * h + d, 3 * D * h + D + d, 3 * D * heads + 2 * D + dims]
    rep = H // KVH
    kcol = [2 * D * (h // rep) + 2 * d, 2 * D * (h // rep) + 2 * (d ^ 1), 2 * D * (heads // rep) + 2 * dims + 1]
    u = np.concatenate([a["L0_ffn_W_exp"].T, a["L0_ffn_b_exp"][:, None]], 1)
    out = {
        "x_nat": x.transpose(1, 0, 2), "x_t": x.reshape(TOK, W).T,
        "wqk0": np.stack([wqkv[:, cols[0]], wqkv[:, cols[1]]], 1), "wv0": wqkv[:, cols[2]],
        "bqk0": np.stack([bqkv[cols[0]], bqkv[cols[1]]], 1), "bv0": bqkv[cols[2]],
        "wproj": a["L0_attn_Wproj"], "bproj": a["L0_attn_bproj"],
        "u0": u.reshape(HC, P, W + 1).transpose(1, 0, 2),
        "d0": a["L0_ffn_W_con"].reshape(HC, P, W).transpose(1, 0, 2),
        "bfw": _butterfly_layout(a["L0_ffn_up_weights"], a["L0_ffn_down_weights"]),
        "bup": a["L0_ffn_up_bias"].reshape(HC, P).T,
        "bcon": a["L0_ffn_b_con"], "bdown": a["L0_ffn_down_bias"],
        "wqa_t": a["L1_attn_Wqa"].T,
        "wqb": np.concatenate([a["L1_attn_Wqb"][:, D * h + d], a["L1_attn_Wqb"][:, D * h + (d ^ 1)]], 1),
        "wkva_t": a["L1_attn_Wkva"].T,
        "wkvb": np.concatenate([a["L1_attn_Wkvb"][:, c] for c in kcol], 1),
        "wout": a["L1_attn_Wout"], "bout": a["L1_attn_bout"],
        "wi_all": np.stack([a["L1_ffn_w_gate"].T, a["L1_ffn_w_up"].T,
                            a["L1_ffn_w_down"].T.reshape(SC, P, W).transpose(1, 0, 2).reshape(P, HS)], 1),
    }
    out.update(_constants())
    return out


_ORDER = ["x_nat", "x_t", "wqk0", "wv0", "bqk0", "bv0", "wproj", "bproj", "u0", "d0", "bfw", "bup", "bcon", "bdown",
          "perms", "wqa_t", "wqb", "wkva_t", "wkvb", "wout", "bout", "rope_c", "rope_s", "wi_all", "ident", "causal"]


def kernel(**inputs):
    import concourse.bacc as bacc
    from concourse.bass_utils import run_bass_kernel_spmd

    arrays = _arrays({k: np.asarray(v) for k, v in inputs.items()})
    arrays = {k: np.ascontiguousarray(arrays[k]) for k in _ORDER}
    nc = bacc.Bacc("TRN2", target_bir_lowering=False, num_devices=1)
    args = [nc.dram_tensor(k, v.shape, mybir.dt.from_np(v.dtype), kind="ExternalInput").ap() for k, v in arrays.items()]
    out = nc.dram_tensor("out", (P, NT, W), mybir.dt.float32, kind="ExternalOutput").ap()
    block_kernel(nc, *args, out)
    res = run_bass_kernel_spmd(nc, [arrays], core_ids=[0]).results[0]["out"]
    return res.transpose(1, 0, 2).reshape(NB, T, W)
```

```python
import numpy as np
import concourse.bass as bass
from concourse import mybir
from contextlib import ExitStack

NB = 8
T = 256
W = 128
P = 128
H = 16
D = W // H
TOK = NB * T
NT = TOK // P
QT = T // P
HU = 512
HC = HU // P
STAGES = 9
INNER = 7
HS = 384
SC = HS // P
QLORA, KVLORA, KVH = 64, 32, 4
PARTS = 3
SROWS = PARTS * PARTS * D
MROW = 96
VP = 32
QH = 4
HEADS = NB * H
QUADS = HEADS // QH
FT = 512
NF = TOK // FT
FS = FT // P
RING = 3
EPS = 1e-5
SCALE = float(D) ** -0.5
MASKED = -1e30
TWO_ONES = float(np.array([0x3F803F80], np.uint32).view(np.float32)[0])

LEAD = 24
AT_QK, AT_QK2, AT_V = -54, -52, -45
AT_SPLIT = (-51, -47, -43, -39)
AT_OUT = -38
AT_IN = (-35, -29)
AT_MT = -7
PV_LAG = 6
MASK_LAG = 4
O_LAG = 10
AT_T, AT_ATT, AT_PROJ, AT_LN, AT_XT = (20, 22), 24, 27, 29, 31
FIRST = AT_QK
BUTTERFLY = (-38, -37, -36, -35, -34, -22, -18, -14, -10)
SHIFT = 168
UP = ([[104, 104, 106, 106], [110, 110, 113, 113],
       [128 + 2 * c for c in range(HC)], [144 + 2 * c for c in range(HC)]],
      [[SHIFT + 128 + f for f in t] for t in ((0, 1, 3), (4, 6, 7), (9, 10, 12), (17, 18, 19))])
BACK = ([109, 116, 137, 153], [SHIFT + 128 + f for f in (5, 9, 14, 21)])
F_LN, F_XT = 2, 4
SLOTS = range(FIRST, SHIFT + 128 + 40)


def last_user(b, ring):
    return max(i for i in range(NB) if i % ring == b % ring)


def at_slot(g, offset, every=H, count=NB):
    n, rest = divmod(g - offset, every)
    return n if rest == 0 and 0 <= n < count else None


def block_kernel(nc, x_nat, x_t, wqk0, wv0, bqk0, bv0, wproj, bproj, u0, d0, bfw, bup, bcon, bdown,
                 perms, wqa_t, wqb, wkva_t, wkvb, wout, bout, rope_c, rope_s, wi_all, ident, causal, out):
    F32, BF, I32 = mybir.dt.float32, mybir.dt.bfloat16, mybir.dt.int32
    ALU = mybir.AluOpType
    ACT = mybir.ActivationFunctionType
    AX = mybir.AxisListType

    scratch = nc.dram_tensor("qk_parts", [2, NB, 2, PARTS, P, T], BF, kind="Internal").ap()

    ctx = ExitStack()
    with ctx:
        def sb(name, shape, dt=F32):
            return ctx.enter_context(nc.sbuf_tensor(name, shape, dt))

        def sem(name):
            return ctx.enter_context(nc.semaphore(name))

        wqk_sb = sb("wqk_sb", [P, 2, W])
        wv_sb = sb("wv_sb", [P, W])
        bqk_sb = sb("bqk_sb", [P, 2])
        bv_sb = sb("bv_sb", [P, W])
        wproj_sb = sb("wproj_sb", [P, W])
        bproj_sb = sb("bproj_sb", [P, W])
        up = [sb(f"up{i}", [P, HC, W + 1]) for i in range(2)]
        down = [sb(f"down{i}", [P, HC, W]) for i in range(2)]
        own = sb("own", [P, 2, HC, W + 1])
        bfw_sb = sb("bfw_sb", [P, 2, STAGES, 2, HC])
        bias4 = sb("bias4", [P, HC])
        perm_sb = sb("perm_sb", [P, INNER, P])
        bup_sb = sb("bup_sb", [P, HC])
        bhid = sb("bhid", [P, HC])
        bcon_sb = sb("bcon_sb", [P, W])
        bdown_sb = sb("bdown_sb", [P, W])
        wup = sb("wup", [P, HU])
        wqa_sb = sb("wqa_sb", [QLORA, W])
        wqb_sb = sb("wqb_sb", [QLORA, 2 * W])
        wkva_sb = sb("wkva_sb", [KVLORA, W])
        wkvb_sb = sb("wkvb_sb", [KVLORA, 3 * W])
        wl1 = sb("wl1", [P, 5, W])
        wout_sb = sb("wout_sb", [P, W])
        bout_sb = sb("bout_sb", [P, W])
        ropec_sb = sb("ropec_sb", [P, 2, T])
        ropes_sb = sb("ropes_sb", [P, 2, T])
        wi = sb("wi", [P, 3, HS], I32)
        wf = sb("wf", [P, 3, HS])
        id32 = sb("id32", [P, P])
        id16 = sb("id16", [P, P], BF)
        mask_sb = sb("mask_sb", [P, T])
        half = sb("half", [P, FS])
        xt = sb("xt", [P, TOK])
        xb = sb("xb", [P, NT, W])
        qk32 = sb("qk32", [P, 2, T])
        rope1 = sb("rope1", [P, 2, T])
        rope2 = sb("rope2", [P, 2, T])
        rest = sb("rest", [P, 2, T])
        parts = sb("parts", [P, 2, PARTS, 2, T], BF)
        Q = sb("Q", [P, 3, H, T], BF)
        K = sb("K", [P, 3, H, T], BF)
        V = sb("V", [P, 4, QT, H, VP])
        mx = sb("mx", [P, 2, QT, H])
        mrest = sb("mrest", [P, QT, H])
        mparts = sb("mparts", [P, QT, PARTS, H], BF)
        mt = sb("mt", [PARTS * H, 2, T], BF)
        E = sb("E", [P, 2, QH, 2 * T])
        O = sb("O", [P, 2, 2, 2, T])
        rec = sb("rec", [P, QT, H])
        at = sb("at", [P, QT, W])
        att = sb("att", [P, T])
        masked_s = sb("masked_s", [P, 2, T + P])
        NA, NFF = [{"r": sb(f"r_{k}", [P, n, W]), "stats": sb(f"stats_{k}", [P, n, 6]), "mv": sb(f"mv_{k}", [P, n, 2]),
                    "ve": sb(f"ve_{k}", [P, n]), "rstd": sb(f"rstd_{k}", [P, n]), "ln": sb(f"ln_{k}", [P, 2, n, W])}
                   for k, n in (("a", QT), ("f", FS))]
        hid = sb("hid", [P, 2, HC, FT])
        sg = sb("sg", [P, 2, FT])

        ST = [ctx.enter_context(nc.psum_tensor(f"ST{i}", [P, 512], F32)) for i in range(RING)]
        SM = [ctx.enter_context(nc.psum_tensor(f"SM{i}", [P, 512], F32)) for i in range(RING)]
        PV = ctx.enter_context(nc.psum_tensor("PV", [P, 512], F32))
        MISC = ctx.enter_context(nc.psum_tensor("MISC", [P, 512], F32))

        ld = {n: sem(f"ld_{n}") for n in ("qk", "x", "v", "id", "perm", "bf", "xb", "proj", "l1", "next", "rope", "gate")}
        clean, v_clean = sem("clean"), sem("v_clean")
        id16_ready = sem("id16_ready")
        swap_ps, own_ready, stage_done = sem("swap_ps"), sem("own_ready"), sem("stage_done")
        wup_ps, wup_ready, bhid_ready = sem("wup_ps"), sem("wup_ready"), sem("bhid_ready")
        wl1_ps, wl1_ready, wf_ready = sem("wl1_ps"), sem("wl1_ready"), sem("wf_ready")
        xb0_ready, bnext_ready = sem("xb0_ready"), sem("bnext_ready")
        pool_chain, dve_chain = sem("pool_chain"), sem("dve_chain")
        AS = [{n: sem(f"a{l}_{n}") for n in (
            "qk_ps", "qk_out", "parts_ready", "wrote", "v_ps", "v_ready", "sm_ps", "max_done",
            "mparts_ready", "mt_ps", "mt_ready", "m_in", "st_ps", "exp_done", "masked", "pv_ps", "o_ready",
            "t_ps", "at_ready", "att_ps", "att_ready", "proj_ps", "res_done", "var_ready", "rstd_ready",
            "ln_ready", "xt_ps", "xt_ready", "xb_ready")} for l in range(2)]
        FF = [{n: sem(f"f{l}_{n}") for n in (
            "up_ps", "sg_ready", "hid_ready", "down_ps", "res_done", "var_ready", "rstd_ready", "ln_ready",
            "xt_ps", "xt_ready", "xb_ready")} for l in range(2)]
        rows_in = [[[sem(f"a{l}_rows_in_{i}{h}") for h in range(2)] for i in range(2)] for l in range(2)]
        stored = [sem(f"stored{i}") for i in range(2)]

        def hidden0(n, c):
            return (SM if n < 2 else ST)[(n * HC + c) % RING][:, :]

        block = ctx.enter_context(nc.Block())

        def over_partitions(vec):
            return vec.rearrange("(a n) -> a n", a=1).broadcast_to([P, W])

        @block.sync
        def _(sp):
            sp.dma_start(xt[:, 0:T], x_t[:, 0:T]).then_inc(ld["x"], 16)
            sp.dma_start(wqk_sb[:, :, :], wqk0).then_inc(ld["qk"], 16)
            sp.dma_start(bqk_sb[:, :], bqk0).then_inc(ld["qk"], 16)
            sp.dma_start(wv_sb[:, :], wv0).then_inc(ld["v"], 16)
            sp.dma_start(bv_sb[:, :], over_partitions(bv0)).then_inc(ld["v"], 16)
            sp.dma_start(perm_sb[:, :, :], perms).then_inc(ld["perm"], 16)
            sp.dma_start(up[0][:, :, :], u0).then_inc(ld["bf"], 16)
            sp.dma_start(down[0][:, :, :], d0).then_inc(ld["bf"], 16)
            sp.dma_start(bfw_sb[:, :, :, :, :], bfw).then_inc(ld["bf"], 16)
            sp.dma_start(bup_sb[:, :], bup).then_inc(ld["bf"], 16)
            sp.dma_start(xt[:, T:TOK], x_t[:, T:TOK]).then_inc(ld["x"], 16)
            sp.dma_start(id32[:, :], ident).then_inc(ld["id"], 16)
            sp.dma_start(mask_sb[:, :], causal).then_inc(ld["id"], 16)

            def late_loads():
                sp.dma_start(xb[:, :, :], x_nat).then_inc(ld["xb"], 16)
                sp.dma_start(bproj_sb[:, :], over_partitions(bproj)).then_inc(ld["xb"], 16)
                for dst, src in ((wqa_sb, wqa_t), (wqb_sb, wqb), (wkva_sb, wkva_t), (wkvb_sb, wkvb)):
                    sp.dma_start(dst[:, :], src).then_inc(ld["l1"], 16)
                sp.dma_start(wproj_sb[:, :], wproj).then_inc(ld["proj"], 16)
                sp.dma_start(wout_sb[:, :], wout).then_inc(ld["next"], 16)
                for dst, src in ((bout_sb, bout), (bcon_sb, bcon), (bdown_sb, bdown)):
                    sp.dma_start(dst[:, :], over_partitions(src)).then_inc(ld["next"], 16)
                sp.dma_start(ropec_sb[:, :, :], rope_c).then_inc(ld["rope"], 16)
                sp.dma_start(ropes_sb[:, :, :], rope_s).then_inc(ld["rope"], 16)
                sp.dma_start(wi[:, :, :], wi_all).then_inc(ld["gate"], 16)

            def attention(l, g):
                S = AS[l]
                if (b := at_slot(g, AT_OUT)) is not None:
                    sp.wait_ge(S["parts_ready"], b + 1)
                    for s in range(2):
                        sp.dma_start(scratch[l, b, s].rearrange("a p t -> p a t"), parts[:, b % 2, :, s, :])\
                            .then_inc(S["wrote"], 16)
                for half_ in range(2):
                    if (b := at_slot(g, AT_IN[half_])) is not None:
                        if half_ == 0:
                            sp.wait_ge(S["wrote"], 32 * (b + 1))
                            if l == 0 and b < 3:
                                sp.wait_ge(clean, 3 * (b + 1))
                        if b >= 3:
                            sp.wait_ge(S["st_ps"], H * (b - 3) + H // 2 * (half_ + 1))
                        elif l == 1:
                            sp.wait_ge(AS[0]["st_ps"], H * (last_user(b, 3) + 1))
                        heads = slice(H // 2 * half_, H // 2 * (half_ + 1))
                        cols = slice(H // 2 * half_ * T, H // 2 * (half_ + 1) * T)
                        done = rows_in[l][b % 2][half_]
                        for a in range(PARTS):
                            sp.dma_start(Q[PARTS * D * a:PARTS * D * (a + 1), b % 3, heads, :],
                                         scratch[l, b, 0, a:a + 1].rearrange("a (d h) t -> a d (h t)", h=H)[:, :, cols]
                                         .broadcast_to([PARTS, D, H // 2 * T])).then_inc(done, 16)
                        sp.dma_start(K[0:SROWS, b % 3, heads, :],
                                     scratch[l, b, 1:2].rearrange("o a (d h) t -> o (a d) (h t)", h=H)[:, :, cols]
                                     .broadcast_to([PARTS, PARTS * D, H // 2 * T])).then_inc(done, 16)
                        if l == 0 and b == 0 and half_ == 1:
                            late_loads()
                if (b := at_slot(g, AT_MT)) is not None:
                    sp.wait_ge(S["mt_ready"], b + 1)
                    for a in range(PARTS):
                        sp.dma_start(Q[MROW + a:MROW + a + 1, b % 3, :, :],
                                     mt[H * a:H * (a + 1), b % 2, :]).then_inc(S["m_in"], 16)

            for g in SLOTS:
                attention(0, g)
                attention(1, g - SHIFT)
                for n in range(NF):
                    if g == BACK[1][n] + F_LN:
                        sp.wait_ge(FF[1]["ln_ready"], n + 1)
                        sp.dma_start(out[:, n * FS:(n + 1) * FS, :], NFF["ln"][:, n % 2, :, :]).then_inc(stored[n % 2], 16)
            for i in range(2):
                sp.wait_ge(stored[i], 16 * NF // 2)

        @block.tensor
        def _(pe):
            misc_read = []

            def misc(semaphore, value):
                if misc_read:
                    pe.wait_ge(*misc_read.pop())
                misc_read.append((semaphore, value))

            def butterfly(k):
                for c, (buf, s) in enumerate(((up, k), (down, STAGES - 1 - k))):
                    if s >= INNER:
                        continue
                    if k == 0:
                        pe.wait_ge(ld["bf"], 64)
                        pe.wait_ge(ld["perm"], 16)
                    else:
                        pe.wait_ge(stage_done, 2 * k)
                    src = buf[k % 2]
                    ins = nc.tensor.matmul(ST[c][:, :], perm_sb[:, s, :], src[:, :, 0:W], start=True, stop=True)
                    if c == 0:
                        ins = nc.tensor.matmul(ST[2][:, 0:HC], perm_sb[:, s, :], src[:, :, W], start=True, stop=True)
                    ins.then_inc(swap_ps, 1)

            def weights():
                pe.wait_ge(stage_done, 2 * STAGES)
                pe.wait_ge(ld["id"], 32)
                for c in range(HC):
                    ins = nc.tensor.transpose(ST[0][:, c * P:(c + 1) * P], up[1][:, c, 0:W], id32[:, :])
                ins.then_inc(wup_ps, 1)
                pe.wait_ge(ld["l1"], 64)
                nc.tensor.matmul(ST[1][:, 0:2 * W], wqa_sb[:, :], wqb_sb[:, :], start=True, stop=True)
                nc.tensor.matmul(ST[2][:, 0:3 * W], wkva_sb[:, :], wkvb_sb[:, :], start=True, stop=True)\
                    .then_inc(wl1_ps, 1)

            def project(l, b, S, first, second):
                tokens = xt[:, b * T:(b + 1) * T]
                nc.tensor.matmul(MISC[:, 0:T], first, tokens, start=True, stop=True)
                nc.tensor.matmul(MISC[:, T:2 * T], second, tokens, start=True, stop=True).then_inc(S["qk_ps"], 1)

            def attention(l, g):
                S = AS[l]
                n_keys = (T, T) if l == 0 else (P, T)
                if (b := at_slot(g, AT_QK)) is not None:
                    misc(S["qk_out"], 2 * b + (2 if l == 0 else 1))
                    if l == 0:
                        if b <= 1:
                            pe.wait_ge(ld["x"], 16 * (b + 1))
                        if b == 0:
                            pe.wait_ge(ld["qk"], 32)
                        project(l, b, S, wqk_sb[:, 0, :], wqk_sb[:, 1, :])
                    else:
                        if b % 2 == 0:
                            pe.wait_ge(FF[0]["xt_ready"], b // 2 + 1)
                        if b == 0:
                            pe.wait_ge(wl1_ready, 2)
                        project(l, b, S, wl1[:, 0, :], wl1[:, 2, :])
                if l == 1 and (b := at_slot(g, AT_QK2)) is not None:
                    misc(S["qk_out"], 2 * b + 2)
                    project(l, b, S, wl1[:, 1, :], wl1[:, 3, :])
                if (b := at_slot(g, AT_V)) is not None:
                    misc(S["v_ready"], b + 1)
                    if l == 0 and b == 0:
                        pe.wait_ge(ld["v"], 32)
                    for k in range(QT):
                        ins = nc.tensor.matmul(MISC[:, k * P:(k + 1) * P], xt[:, b * T + k * P:b * T + (k + 1) * P],
                                               wv_sb[:, :] if l == 0 else wl1[:, 4, :], start=True, stop=True)
                    ins.then_inc(S["v_ps"], 1)
                if l == 0 and g in BUTTERFLY:
                    butterfly(BUTTERFLY.index(g))
                if l == 0 and g == -8:
                    weights()
                m = g + LEAD
                if 0 <= m < HEADS:
                    b, h = divmod(m, H)
                    if h % (H // 2) == 0:
                        pe.wait_ge(rows_in[l][b % 2][h // (H // 2)], 64 * (b // 2 + 1))
                    if l == 1 and m == 0:
                        pe.wait_ge(FF[0]["hid_ready"], 2 * HC)
                    if m >= RING:
                        pe.wait_ge(S["max_done"], m - RING + 1)
                    bank = SM[m % RING]
                    if l == 0:
                        for q in range(QT):
                            ins = nc.tensor.matmul(bank[:, q * T:(q + 1) * T], Q[0:MROW, b % 3, h, q * P:(q + 1) * P],
                                                   K[0:MROW, b % 3, h, :], start=True, stop=True)
                    else:
                        nc.tensor.matmul(bank[:, 0:T], Q[0:MROW, b % 3, h, P:T], K[0:MROW, b % 3, h, :],
                                         start=True, stop=True)
                        ins = nc.tensor.matmul(bank[:, T:T + P], Q[0:MROW, b % 3, h, 0:P], K[0:MROW, b % 3, h, 0:P],
                                               start=True, stop=True)
                    ins.then_inc(S["sm_ps"], 1)
                if (b := at_slot(g, AT_MT)) is not None:
                    misc(S["mt_ready"], b + 1)
                    if l == 0 and b == 0:
                        pe.wait_ge(id16_ready, 1)
                    pe.wait_ge(S["mparts_ready"], b + 1)
                    for q in range(QT):
                        ins = nc.tensor.transpose(MISC[:, :].bitcast(BF)[0:PARTS * H, q * P:(q + 1) * P],
                                                  mparts[:, q, :, :], id16[:, :])
                    ins.then_inc(S["mt_ps"], 1)
                if 0 <= g < HEADS:
                    b, h = divmod(g, H)
                    if h == 0:
                        pe.wait_ge(S["m_in"], 48 * (b + 1))
                    if l == 0 and g == 0:
                        pe.wait_ge(wl1_ready, 2)
                        pe.wait_ge(wup_ready, 1)
                    if l == 1 and g == 0:
                        pe.wait_ge(FF[0]["hid_ready"], NF * HC)
                    if g >= RING:
                        pe.wait_ge(S["exp_done"], g - RING + 1)
                    bank = ST[g % RING]
                    for k in range(QT):
                        q0 = k * P if l == 1 else 0
                        ins = nc.tensor.matmul(bank[:, k * T:(k + 1) * T - q0], K[:, b % 3, h, k * P:(k + 1) * P],
                                               Q[:, b % 3, h, q0:T], start=True, stop=True)
                    ins.then_inc(S["st_ps"], 1)
                if (a := at_slot(g, PV_LAG, QH, QUADS)) is not None:
                    b, r4 = divmod(a, H // QH)
                    if l == 0:
                        pe.wait_ge(S["exp_done"], QH * (a + 1))
                    else:
                        pe.wait_ge(S["masked"], 2 * (a + 1))
                    if r4 == 0:
                        pe.wait_ge(S["v_ready"], b + 1)
                    if a % 2 == 0 and a:
                        pe.wait_ge(S["o_ready"], a // 2)
                    elif l == 1 and a == 0:
                        pe.wait_ge(AS[0]["o_ready"], QUADS // 2)
                    for k in range(QT):
                        q0 = k * P if l == 1 else 0
                        for j in range(QH):
                            ins = nc.tensor.matmul(PV[VP * j:VP * (j + 1), a % 2 * T + q0:(a % 2 + 1) * T],
                                                   V[:, b % 4, k, QH * r4 + j, :], E[:, a % 2, j, k * T:(k + 1) * T - q0],
                                                   start=(k == 0), stop=(k == QT - 1))
                    ins.then_inc(S["pv_ps"], 1)
                for q in range(QT):
                    if (b := at_slot(g, AT_T[q])) is not None:
                        misc(S["at_ready"], QT * b + q + 1)
                        pe.wait_ge(S["o_ready"], 2 * (b + 1))
                        if l == 0 and b == 0:
                            pe.wait_ge(ld["id"], 32)
                        for a in range(H // QH):
                            ins = nc.tensor.transpose(MISC[:, a * P:(a + 1) * P],
                                                      O[:, b % 2, a // 2, a % 2, q * P:(q + 1) * P], id32[:, :])
                        ins.then_inc(S["t_ps"], 1)
                if (b := at_slot(g, AT_ATT)) is not None:
                    misc(S["att_ready"], b + 1)
                    pe.wait_ge(S["at_ready"], QT * (b + 1))
                    for q in range(QT):
                        ins = nc.tensor.transpose(MISC[:, q * P:(q + 1) * P], at[:, q, :], id32[:, :])
                    ins.then_inc(S["att_ps"], 1)
                if (b := at_slot(g, AT_PROJ)) is not None:
                    misc(S["res_done"], b + 1)
                    pe.wait_ge(S["att_ready"], b + 1)
                    if b == 0:
                        pe.wait_ge(ld["proj" if l == 0 else "next"], 16 if l == 0 else 64)
                    for q in range(QT):
                        ins = nc.tensor.matmul(MISC[:, q * P:(q + 1) * P], att[:, q * P:(q + 1) * P],
                                               (wproj_sb if l == 0 else wout_sb)[:, :], start=True, stop=True)
                    ins.then_inc(S["proj_ps"], 1)
                if (b := at_slot(g, AT_XT)) is not None:
                    misc(S["xt_ready"], b + 1)
                    pe.wait_ge(S["ln_ready"], b + 1)
                    for q in range(QT):
                        ins = nc.tensor.transpose(MISC[:, q * P:(q + 1) * P], NA["ln"][:, b % 2, q, :], id32[:, :])
                    ins.then_inc(S["xt_ps"], 1)

            def ffn(l, g):
                F = FF[l]
                C = HC if l == 0 else SC
                for n in range(NF):
                    for c in range(C):
                        if UP[l][n][c] != g:
                            continue
                        m = n * C + c
                        tokens = xt[:, n * FT:(n + 1) * FT]
                        if c == 0:
                            pe.wait_ge(AS[l]["xt_ready"], 2 * (n + 1))
                        if l == 0:
                            if m == 0:
                                pe.wait_ge(AS[0]["max_done"], HEADS)
                            elif m == 2 * HC:
                                pe.wait_ge(AS[0]["exp_done"], HEADS)
                            if m % (2 * HC) >= RING:
                                pe.wait_ge(F["hid_ready"], m - RING + 1)
                            nc.tensor.matmul(hidden0(n, c), wup[:, c * P:(c + 1) * P], tokens,
                                             start=True, stop=True).then_inc(F["up_ps"], 1)
                        else:
                            if m == 0:
                                pe.wait_ge(wf_ready, 1)
                                pe.wait_ge(AS[1]["exp_done"], HEADS)
                                pe.wait_ge(AS[1]["max_done"], HEADS)
                            elif m >= 2:
                                pe.wait_ge(F["hid_ready"], m - 1)
                            for j, bank in enumerate((ST, SM)):
                                nc.tensor.matmul(bank[m % 2][:, :], wf[:, j, c * P:(c + 1) * P], tokens,
                                                 start=True, stop=True).then_inc(F["up_ps"], 1)
                    if BACK[l][n] == g:
                        if l == 0:
                            misc(F["res_done"], n + 1)
                            if n == 0:
                                pe.wait_ge(stage_done, 2 * STAGES)
                        elif n >= 2:
                            pe.wait_ge(F["res_done"], n - 1)
                        pe.wait_ge(F["hid_ready"], C * (n + 1))
                        bank = MISC if l == 0 else (ST, SM)[n % 2][2]
                        for s in range(FS):
                            for c in range(C):
                                w = down[1][:, c, :] if l == 0 else wf[:, 2, c * W:(c + 1) * W]
                                ins = nc.tensor.matmul(bank[:, s * W:(s + 1) * W], hid[:, n % 2, c, s * P:(s + 1) * P], w,
                                                       start=(c == 0), stop=(c == C - 1))
                        ins.then_inc(F["down_ps"], 1)
                    if l == 0 and BACK[l][n] + F_XT == g:
                        misc(F["xt_ready"], n + 1)
                        pe.wait_ge(F["ln_ready"], n + 1)
                        for s in range(FS):
                            ins = nc.tensor.transpose(MISC[:, s * P:(s + 1) * P], NFF["ln"][:, n % 2, s, :], id32[:, :])
                        ins.then_inc(F["xt_ps"], 1)

            for g in SLOTS:
                attention(0, g)
                ffn(0, g)
                attention(1, g - SHIFT)
                ffn(1, g)

        @block.scalar
        def _(act):
            def attention(l, g):
                S = AS[l]
                if l == 0 and (b := at_slot(g, AT_QK)) is not None:
                    if b == 0:
                        act.wait_ge(ld["qk"], 32)
                    else:
                        act.wait_ge(S["parts_ready"], b)
                    act.wait_ge(S["qk_ps"], b + 1)
                    for s in range(2):
                        act.activation(qk32[:, s, :], MISC[:, s * T:(s + 1) * T], ACT.Identity,
                                       bias=bqk_sb[:, s:s + 1]).then_inc(S["qk_out"], 1)
                if l == 1 and (b := at_slot(g, AT_V)) is not None:
                    act.wait_ge(S["v_ps"], b + 1)
                    if b >= 4:
                        act.wait_ge(S["pv_ps"], H // QH * (b - 3))
                    else:
                        act.wait_ge(AS[0]["pv_ps"], H // QH * (last_user(b, 4) + 1))
                    act.activation(V[:, b % 4, :, :, 0:D], MISC[:, 0:T].rearrange("p (k h d) -> p k h d", k=QT, h=H), ACT.Copy)\
                        .then_inc(S["v_ready"], 1)
                if l == 0 and g == -8:
                    act.wait_ge(wup_ps, 1)
                    act.activation(wup[:, :], ST[0][:, :], ACT.Copy).then_inc(wup_ready, 1)
                    act.wait_ge(wl1_ps, 1)
                    act.activation(wl1[:, 0:2, :], ST[1][:, 0:2 * W], ACT.Copy).then_inc(wl1_ready, 1)
                    act.activation(wl1[:, 2:5, :], ST[2][:, 0:3 * W], ACT.Copy).then_inc(wl1_ready, 1)
                if (b := at_slot(g, AT_MT)) is not None:
                    act.wait_ge(S["mt_ps"], b + 1)
                    if b >= 2:
                        act.wait_ge(S["m_in"], 48 * (b - 1))
                    elif l == 1:
                        act.wait_ge(AS[0]["m_in"], 48 * NB)
                    act.activation(mt[:, b % 2, :], MISC[:, :].bitcast(BF)[0:PARTS * H, 0:T], ACT.Copy)\
                        .then_inc(S["mt_ready"], 1)
                if 0 <= g < HEADS:
                    a, j = divmod(g, QH)
                    act.wait_ge(S["st_ps"], g + 1)
                    if a >= 2:
                        act.wait_ge(S["pv_ps"], a - 1)
                    elif l == 1:
                        act.wait_ge(AS[0]["pv_ps"], QUADS)
                    n = 2 * T if l == 0 else T + P
                    act.activation(E[:, a % 2, j, 0:n], ST[g % RING][:, 0:n], ACT.Exp, scale=SCALE)\
                        .then_inc(S["exp_done"], 1)
                if (n := at_slot(g, O_LAG, 2 * QH, QUADS // 2)) is not None:
                    b = n // 2
                    act.wait_ge(S["pv_ps"], 2 * (n + 1))
                    if b >= 2:
                        act.wait_ge(S["t_ps"], QT * (b - 1))
                    elif l == 1:
                        act.wait_ge(AS[0]["t_ps"], QT * NB)
                    act.activation(O[:, b % 2, n % 2, :, :], PV[:, :], ACT.Copy).then_inc(S["o_ready"], 1)
                if (b := at_slot(g, AT_ATT)) is not None:
                    act.wait_ge(S["att_ps"], b + 1)
                    if b:
                        act.wait_ge(S["proj_ps"], b)
                    elif l == 1:
                        act.wait_ge(AS[0]["proj_ps"], NB)
                    act.activation(att[:, :], MISC[:, 0:T], ACT.Copy).then_inc(S["att_ready"], 1)
                if (b := at_slot(g, AT_XT)) is not None:
                    act.wait_ge(S["xt_ps"], b + 1)
                    act.activation(xt[:, b * T:(b + 1) * T], MISC[:, 0:T], ACT.Copy).then_inc(S["xt_ready"], 1)

            def ffn(l, g):
                F = FF[l]
                C = HC if l == 0 else SC
                for n in range(NF):
                    for c in range(C):
                        if UP[l][n][c] != g:
                            continue
                        m = n * C + c
                        if l == 0:
                            if m == 0:
                                act.wait_ge(bhid_ready, 1)
                            if n >= 2:
                                act.wait_ge(F["down_ps"], n - 1)
                            act.wait_ge(F["up_ps"], m + 1)
                            act.activation(hid[:, n % 2, c, :], hidden0(n, c), ACT.Gelu, bias=bhid[:, c:c + 1])\
                                .then_inc(F["hid_ready"], 1)
                        else:
                            act.wait_ge(F["up_ps"], 2 * m + 1)
                            if m >= 2:
                                act.wait_ge(F["hid_ready"], m - 1)
                            act.activation(sg[:, m % 2, :], ST[m % 2][:, :], ACT.Silu).then_inc(F["sg_ready"], 1)
                    if l == 0 and BACK[l][n] + F_XT == g:
                        act.wait_ge(F["xt_ps"], n + 1)
                        act.activation(xt[:, n * FT:(n + 1) * FT], MISC[:, :], ACT.Copy).then_inc(F["xt_ready"], 1)

            for g in SLOTS:
                attention(0, g)
                ffn(0, g)
                attention(1, g - SHIFT)
                ffn(1, g)

        @block.vector
        def _(dve):
            links, swaps = [0], [0]

            def link(ins):
                links[0] += 1
                ins.then_inc(dve_chain, 1)
                dve.wait_ge(dve_chain, links[0])

            def butterfly(k):
                for c, (buf, s) in enumerate(((up, k), (down, STAGES - 1 - k))):
                    src, dst = buf[k % 2], buf[(k + 1) % 2]
                    w = bfw_sb[:, c, s, 1, :]
                    if k == 0 and c == 0:
                        dve.wait_ge(ld["bf"], 64)
                    elif k:
                        dve.wait_ge(stage_done, 2 * k)
                    if s < INNER:
                        swaps[0] += 1
                        dve.wait_ge(swap_ps, swaps[0])
                    dve.wait_ge(own_ready, 2 * k + c + 1)
                    for ch in range(HC):
                        if s < INNER:
                            partner = ST[c][:, ch * P:(ch + 1) * P]
                        else:
                            partner = src[:, ch ^ (1 << (s - INNER)), 0:W]
                        ins = nc.vector.scalar_tensor_tensor(out=dst[:, ch, 0:W], in0=partner, scalar=w[:, ch:ch + 1],
                                                             in1=own[:, c, ch, 0:W], op0=ALU.mult, op1=ALU.add)
                    if c == 0:
                        if s < INNER:
                            link(nc.vector.tensor_tensor(bias4[:, :], ST[2][:, 0:HC], w, ALU.mult))
                        else:
                            step = 1 << (s - INNER)
                            for ch in range(HC):
                                o = ch ^ step
                                ins = nc.vector.tensor_tensor(bias4[:, ch:ch + 1], src[:, o, W:W + 1], w[:, ch:ch + 1], ALU.mult)
                            link(ins)
                        ins = nc.vector.tensor_tensor(dst[:, :, W], bias4[:, :], own[:, c, :, W], ALU.add)
                    ins.then_inc(stage_done, 1)

            def statistics(N, n, var_ready):
                for s in range(n):
                    ins = nc.vector.bn_stats(N["stats"][:, s, :], N["r"][:, s, :])
                link(ins)
                for s in range(n):
                    ins = nc.vector.bn_aggr(N["mv"][:, s, :], N["stats"][:, s, :])
                link(ins)
                nc.vector.tensor_scalar(N["ve"][:, :], N["mv"][:, :, 1], EPS, None, ALU.add).then_inc(var_ready, 1)

            def normalise(N, n, parity, ln_ready):
                for s in range(n):
                    ins = nc.vector.tensor_scalar(N["ln"][:, parity, s, :], N["r"][:, s, :], N["mv"][:, s, 0:1],
                                                  N["rstd"][:, s:s + 1], ALU.subtract, ALU.mult)
                ins.then_inc(ln_ready, 1)

            def attention(l, g):
                S = AS[l]
                if l == 1:
                    for s, offset in enumerate((AT_QK, AT_QK2)):
                        if (b := at_slot(g, offset)) is not None:
                            if b == 0 and s == 0:
                                dve.wait_ge(ld["rope"], 32)
                            if b:
                                dve.wait_ge(S["parts_ready"], b)
                            dve.wait_ge(S["qk_ps"], 2 * b + s + 1)
                            nc.vector.tensor_tensor((rope1, rope2)[s][:, :, :], MISC[:, :].rearrange("p (s t) -> p s t", s=2),
                                                    (ropec_sb, ropes_sb)[s][:, :, :], ALU.mult).then_inc(S["qk_out"], 1)
                if l == 0 and (b := at_slot(g, AT_V)) is not None:
                    dve.wait_ge(S["v_ps"], b + 1)
                    if b == 0:
                        dve.wait_ge(ld["v"], 32)
                        dve.wait_ge(v_clean, 2)
                    if b >= 4:
                        dve.wait_ge(S["pv_ps"], H // QH * (b - 3))
                    values = V[:, b % 4, :, :, 0:D]
                    found = MISC[:, 0:T].rearrange("p (k h d) -> p k h d", k=QT, h=H)
                    for k in range(QT):
                        ins = nc.vector.tensor_tensor(values[:, k], found[:, k],
                                                      bv_sb[:, :].rearrange("p (h d) -> p h d", h=H), ALU.add)
                    ins.then_inc(S["v_ready"], 1)
                if l == 0 and g == BUTTERFLY[4] + 1:
                    dve.wait_ge(ld["id"], 32)
                    nc.vector.tensor_copy(id16[:, :], id32[:, :]).then_inc(id16_ready, 1)
                if l == 0 and g in BUTTERFLY:
                    butterfly(BUTTERFLY.index(g))
                if l == 0 and g == -8:
                    dve.wait_ge(stage_done, 2 * STAGES)
                    nc.vector.tensor_tensor(bhid[:, :], up[1][:, :, W], bup_sb[:, :], ALU.add).then_inc(bhid_ready, 1)
                m = g + LEAD
                if 0 <= m < HEADS:
                    b, h = divmod(m, H)
                    dve.wait_ge(S["sm_ps"], m + 1)
                    bank = SM[m % RING]
                    if l == 0:
                        ins = nc.vector.tensor_reduce(mx[:, b % 2, :, h], bank[:, :].rearrange("p (q k) -> p q k", q=QT),
                                                      AX.X, ALU.max, negate=True)
                    else:
                        if m >= 2:
                            dve.wait_ge(S["max_done"], m - 1)
                        for q, lo, hi in ((1, 0, T), (0, T, T + P)):
                            ins = nc.vector.tensor_tensor_reduce(
                                out=masked_s[:, m % 2, lo:hi], in0=bank[:, lo:hi], in1=mask_sb[:, T + lo - hi:T], scale=-1.0,
                                scalar=3.0e38, op0=ALU.add, op1=ALU.min, accum_out=mx[:, b % 2, q, h:h + 1])
                    ins.then_inc(S["max_done"], 1)
                    if h == H - 1:
                        dve.wait_ge(S["max_done"], m + 1)
                        if b:
                            dve.wait_ge(S["mt_ps"], b)
                        elif l == 1:
                            dve.wait_ge(AS[0]["mt_ps"], NB)
                        link(nc.vector.tensor_copy(mparts[:, :, 0, :], mx[:, b % 2, :, :]))
                        link(nc.vector.tensor_tensor(mrest[:, :, :], mx[:, b % 2, :, :], mparts[:, :, 0, :], ALU.subtract))
                        link(nc.vector.tensor_copy(mparts[:, :, 1, :], mrest[:, :, :]))
                        nc.vector.tensor_tensor(mparts[:, :, 2, :], mrest[:, :, :], mparts[:, :, 1, :], ALU.subtract)\
                            .then_inc(S["mparts_ready"], 1)
                for q in range(QT):
                    if (b := at_slot(g, AT_T[q])) is not None:
                        dve.wait_ge(S["t_ps"], QT * b + q + 1)
                        found = MISC[:, :].rearrange("p (h c) -> p h c", h=H)
                        link(nc.vector.reciprocal(rec[:, q, :], found[:, :, D]))
                        if b and q == 0:
                            dve.wait_ge(S["att_ps"], b)
                        elif l == 1 and b == 0:
                            dve.wait_ge(AS[0]["att_ps"], NB)
                        nc.vector.tensor_tensor(at[:, q, :].rearrange("p (h d) -> p h d", h=H), found[:, :, 0:D],
                                                rec[:, q, :].unsqueeze(2).broadcast_to([P, H, D]), ALU.mult)\
                            .then_inc(S["at_ready"], 1)
                if (b := at_slot(g, AT_PROJ)) is not None:
                    dve.wait_ge(S["proj_ps"], b + 1)
                    if l == 0 and b == 0:
                        dve.wait_ge(xb0_ready, 1)
                    if l == 1 and b % 2 == 0:
                        dve.wait_ge(FF[0]["xb_ready"], b // 2 + 1)
                    if b:
                        dve.wait_ge(S["ln_ready"], b)
                    elif l == 1:
                        dve.wait_ge(AS[0]["ln_ready"], NB)
                    nc.vector.tensor_tensor(NA["r"][:, :, :], MISC[:, 0:T].rearrange("p (q w) -> p q w", q=QT),
                                            xb[:, QT * b:QT * (b + 1), :], ALU.add).then_inc(S["res_done"], 1)
                    dve.wait_ge(S["res_done"], b + 1)
                    statistics(NA, QT, S["var_ready"])
                if (b := at_slot(g, AT_LN)) is not None:
                    dve.wait_ge(S["rstd_ready"], b + 1)
                    if b >= 2:
                        dve.wait_ge(S["xt_ps"], b - 1)
                        dve.wait_ge(S["xb_ready"], b - 1)
                    elif l == 1:
                        dve.wait_ge(AS[0]["xt_ps"], NB)
                        dve.wait_ge(AS[0]["xb_ready"], NB)
                    normalise(NA, QT, b % 2, S["ln_ready"])

            def ffn(l, g):
                F = FF[l]
                for n in range(NF):
                    for c in range(SC):
                        if l == 1 and UP[l][n][c] == g:
                            m = n * SC + c
                            if c == 0 and n >= 2:
                                dve.wait_ge(F["down_ps"], n - 1)
                            elif m == 0:
                                dve.wait_ge(FF[0]["down_ps"], NF)
                            dve.wait_ge(F["sg_ready"], m + 1)
                            dve.wait_ge(F["up_ps"], 2 * (m + 1))
                            nc.vector.tensor_tensor(hid[:, n % 2, c, :], SM[m % 2][:, :], sg[:, m % 2, :], ALU.mult)\
                                .then_inc(F["hid_ready"], 1)
                    if BACK[l][n] == g:
                        dve.wait_ge(F["down_ps"], n + 1)
                        dve.wait_ge(AS[l]["xb_ready"], 2 * (n + 1))
                        if n:
                            dve.wait_ge(F["ln_ready"], n)
                        elif l == 1:
                            dve.wait_ge(FF[0]["ln_ready"], NF)
                        bank = MISC if l == 0 else (ST, SM)[n % 2][2]
                        nc.vector.tensor_tensor(NFF["r"][:, :, :], bank[:, :].rearrange("p (q w) -> p q w", q=FS),
                                                xb[:, FS * n:FS * (n + 1), :], ALU.add).then_inc(F["res_done"], 1)
                        dve.wait_ge(F["res_done"], n + 1)
                        statistics(NFF, FS, F["var_ready"])
                    if BACK[l][n] + F_LN == g:
                        dve.wait_ge(F["rstd_ready"], n + 1)
                        if l == 0 and n >= 2:
                            dve.wait_ge(F["xt_ps"], n - 1)
                            dve.wait_ge(F["xb_ready"], n - 1)
                        elif l == 1 and n < 2:
                            dve.wait_ge(FF[0]["xt_ps"], NF)
                            dve.wait_ge(FF[0]["xb_ready"], NF)
                        elif l == 1:
                            dve.wait_ge(stored[n % 2], 16 * (n // 2))
                        normalise(NFF, FS, n % 2, F["ln_ready"])

            nc.vector.memset(V[:, :, :, :, :], 0.0).then_inc(v_clean, 1)
            dve.wait_ge(v_clean, 1)
            nc.vector.memset(V[:, :, :, :, D:D + 1], 1.0).then_inc(v_clean, 1)
            for g in SLOTS:
                attention(0, g)
                ffn(0, g)
                attention(1, g - SHIFT)
                ffn(1, g)

        @block.gpsimd
        def _(pool):
            links = [0]

            def link(ins):
                links[0] += 1
                ins.then_inc(pool_chain, 1)
                pool.wait_ge(pool_chain, links[0])

            def split(l, b, step):
                S = AS[l]
                p = parts[:, b % 2]
                if step == 0:
                    pool.wait_ge(S["qk_out"], 2 * (b + 1))
                    if l == 1:
                        if b:
                            pool.wait_ge(S["parts_ready"], b)
                        link(nc.gpsimd.tensor_tensor(qk32[:, :, :], rope1[:, :, :], rope2[:, :, :], ALU.add))
                elif step == 1:
                    if b >= 2:
                        pool.wait_ge(S["wrote"], 32 * (b - 1))
                    elif l == 1:
                        pool.wait_ge(AS[0]["wrote"], 32 * NB)
                    link(nc.gpsimd.tensor_scalar(p[:, 0], qk32[:, :, :], 1.0, 0.0, ALU.mult, ALU.add))
                    link(nc.gpsimd.tensor_tensor(rest[:, :, :], qk32[:, :, :], p[:, 0], ALU.subtract))
                elif step == 2:
                    link(nc.gpsimd.tensor_scalar(p[:, 1], rest[:, :, :], 1.0, 0.0, ALU.mult, ALU.add))
                else:
                    nc.gpsimd.tensor_tensor(p[:, 2], rest[:, :, :], p[:, 1], ALU.subtract).then_inc(S["parts_ready"], 1)

            def butterfly(k):
                for c, (buf, s, n) in enumerate(((up, k, W + 1), (down, STAGES - 1 - k, W))):
                    if k == 0 and c == 0:
                        pool.wait_ge(ld["bf"], 64)
                    elif k:
                        pool.wait_ge(stage_done, 2 * (k - 1) + c + 1)
                    nc.gpsimd.tensor_tensor(own[:, c, :, 0:n], buf[k % 2][:, :, 0:n],
                                            bfw_sb[:, c, s, 0, :].unsqueeze(2).broadcast_to([P, HC, n]), ALU.mult)\
                        .then_inc(own_ready, 1)

            def attention(l, g):
                S = AS[l]
                if l == 1 and (a := at_slot(g, MASK_LAG, QH, QUADS)) is not None:
                    pool.wait_ge(S["exp_done"], QH * (a + 1))
                    for c in (0, T):
                        e = E[:, a % 2, :, c:c + P]
                        nc.gpsimd.affine_select(out=e, in_=e, pattern=[[0, QH], [1, P]], compare_op=ALU.is_ge,
                                                fill=0.0, base=0, channel_multiplier=-1).then_inc(S["masked"], 1)
                for step in range(len(AT_SPLIT)):
                    if (b := at_slot(g, AT_SPLIT[step])) is not None:
                        split(l, b, step)
                if l == 0 and g in BUTTERFLY:
                    butterfly(BUTTERFLY.index(g))
                if l == 0 and g in (-33, -26):
                    clear(1 if g == -33 else 2)
                if l == 0 and g == -4:
                    pool.wait_ge(ld["xb"], 32)
                    nc.gpsimd.tensor_tensor(xb[:, :, :], xb[:, :, :],
                                            bproj_sb[:, :].unsqueeze(1).broadcast_to([P, NT, W]), ALU.add)\
                        .then_inc(xb0_ready, 1)
                    pool.wait_ge(ld["next"], 64)
                    nc.gpsimd.tensor_tensor(bcon_sb[:, :], bcon_sb[:, :], bdown_sb[:, :], ALU.add)\
                        .then_inc(bnext_ready, 1)
                if l == 0 and g == 12:
                    pool.wait_ge(ld["gate"], 16)
                    nc.gpsimd.tensor_scalar(wf[:, :, :], wi[:, :, :], 1.0 / 127.0, 0.0, ALU.mult, ALU.add).then_inc(wf_ready, 1)
                if (b := at_slot(g, AT_PROJ)) is not None:
                    pool.wait_ge(S["var_ready"], b + 1)
                    nc.gpsimd.tensor_tensor(NA["rstd"][:, :], NA["ve"][:, :], half[:, 0:QT], ALU.pow).then_inc(S["rstd_ready"], 1)
                if (b := at_slot(g, AT_LN)) is not None:
                    pool.wait_ge(S["ln_ready"], b + 1)
                    dst, src = xb[:, QT * b:QT * (b + 1), :], NA["ln"][:, b % 2, :, :]
                    if l == 0:
                        if b == 0:
                            pool.wait_ge(bnext_ready, 1)
                        nc.gpsimd.tensor_tensor(dst, src, bcon_sb[:, :].unsqueeze(1).broadcast_to([P, QT, W]), ALU.add)\
                            .then_inc(S["xb_ready"], 1)
                    else:
                        nc.gpsimd.tensor_scalar(dst, src, 1.0, 0.0, ALU.mult, ALU.add).then_inc(S["xb_ready"], 1)

            def ffn(l, g):
                F = FF[l]
                for n in range(NF):
                    if BACK[l][n] == g:
                        pool.wait_ge(F["var_ready"], n + 1)
                        nc.gpsimd.tensor_tensor(NFF["rstd"][:, :], NFF["ve"][:, :], half[:, :], ALU.pow)\
                            .then_inc(F["rstd_ready"], 1)
                    if l == 0 and BACK[l][n] + F_LN == g:
                        pool.wait_ge(F["ln_ready"], n + 1)
                        nc.gpsimd.tensor_tensor(xb[:, FS * n:FS * (n + 1), :], NFF["ln"][:, n % 2, :, :],
                                                bout_sb[:, :].unsqueeze(1).broadcast_to([P, FS, W]), ALU.add)\
                            .then_inc(F["xb_ready"], 1)

            def clear(i):
                if i:
                    pool.wait_ge(own_ready, 2 * 5)
                for x in (Q, K):
                    nc.gpsimd.memset(x[64:P, i, :, :].bitcast(F32), 0.0).then_inc(clean, 1)
                pool.wait_ge(clean, 3 * i + 2)
                nc.gpsimd.memset(K[MROW:MROW + PARTS, i, :, :].bitcast(F32), TWO_ONES).then_inc(clean, 1)
                pool.wait_ge(clean, 3 * i + 3)

            link(nc.gpsimd.memset(half[:, :], -0.5))
            clear(0)
            for g in SLOTS:
                attention(0, g)
                ffn(0, g)
                attention(1, g - SHIFT)
                ffn(1, g)


def _features():
    d, h = np.meshgrid(np.arange(D), np.arange(H), indexing="ij")
    return d.ravel(), h.ravel()


def _constants():
    d, _ = _features()
    inv = (1.0 / np.float32(10000.0) ** (np.arange(0, D, 2, dtype=np.float32) / np.float32(D))).astype(np.float32)
    freqs = np.outer(np.arange(T, dtype=np.float32), inv).astype(np.float32)
    c = np.cos(freqs).astype(np.float32).T[d // 2]
    s = np.sin(freqs).astype(np.float32).T[d // 2] * np.where(d % 2 == 0, -1.0, 1.0).astype(np.float32)[:, None]
    i = np.arange(P)
    perms = np.zeros((P, INNER, P), np.float32)
    for k in range(INNER):
        perms[i, k, i ^ (1 << k)] = 1.0
    later = np.where(i[None, :] > i[:, None], np.float32(MASKED), np.float32(0.0))
    return {
        "rope_c": np.stack([c, c], 1), "rope_s": np.stack([s, s], 1), "perms": perms,
        "ident": np.eye(P, dtype=np.float32), "causal": np.concatenate([later, later], 1).astype(np.float32),
    }


def _butterfly_layout(up_weights, down_weights):
    f = np.arange(HU)
    out = np.empty((HU, 2, STAGES, 2), np.float32)
    for s in range(STAGES):
        k, j = (f >> (s + 1) << s) + f % (1 << s), f >> s & 1
        out[:, 0, s, 0], out[:, 0, s, 1] = up_weights[s, k, j, j], up_weights[s, k, j, 1 - j]
        out[:, 1, s, 0], out[:, 1, s, 1] = down_weights[s, k, j, j], down_weights[s, k, 1 - j, j]
    return out.reshape(HC, P, 2, STAGES, 2).transpose(1, 2, 3, 4, 0)


def _arrays(a):
    d, h = _features()
    wqkv, bqkv = a["L0_attn_Wqkv"], a["L0_attn_bqkv"]
    x = a["L0_attn_x"].reshape(NT, P, W)
    heads, dims = np.arange(W) // D, np.arange(W) % D
    cols = [3 * D * h + d, 3 * D * h + D + d, 3 * D * heads + 2 * D + dims]
    rep = H // KVH
    kcol = [2 * D * (h // rep) + 2 * d, 2 * D * (h // rep) + 2 * (d ^ 1), 2 * D * (heads // rep) + 2 * dims + 1]
    u = np.concatenate([a["L0_ffn_W_exp"].T, a["L0_ffn_b_exp"][:, None]], 1)
    out = {
        "x_nat": x.transpose(1, 0, 2), "x_t": x.reshape(TOK, W).T,
        "wqk0": np.stack([wqkv[:, cols[0]], wqkv[:, cols[1]]], 1), "wv0": wqkv[:, cols[2]],
        "bqk0": np.stack([bqkv[cols[0]], bqkv[cols[1]]], 1), "bv0": bqkv[cols[2]],
        "wproj": a["L0_attn_Wproj"], "bproj": a["L0_attn_bproj"],
        "u0": u.reshape(HC, P, W + 1).transpose(1, 0, 2),
        "d0": a["L0_ffn_W_con"].reshape(HC, P, W).transpose(1, 0, 2),
        "bfw": _butterfly_layout(a["L0_ffn_up_weights"], a["L0_ffn_down_weights"]),
        "bup": a["L0_ffn_up_bias"].reshape(HC, P).T,
        "bcon": a["L0_ffn_b_con"], "bdown": a["L0_ffn_down_bias"],
        "wqa_t": a["L1_attn_Wqa"].T,
        "wqb": np.concatenate([a["L1_attn_Wqb"][:, D * h + d], a["L1_attn_Wqb"][:, D * h + (d ^ 1)]], 1),
        "wkva_t": a["L1_attn_Wkva"].T,
        "wkvb": np.concatenate([a["L1_attn_Wkvb"][:, c] for c in kcol], 1),
        "wout": a["L1_attn_Wout"], "bout": a["L1_attn_bout"],
        "wi_all": np.stack([a["L1_ffn_w_gate"].T, a["L1_ffn_w_up"].T,
                            a["L1_ffn_w_down"].T.reshape(SC, P, W).transpose(1, 0, 2).reshape(P, HS)], 1),
    }
    out.update(_constants())
    return out


_ORDER = ["x_nat", "x_t", "wqk0", "wv0", "bqk0", "bv0", "wproj", "bproj", "u0", "d0", "bfw", "bup", "bcon", "bdown",
          "perms", "wqa_t", "wqb", "wkva_t", "wkvb", "wout", "bout", "rope_c", "rope_s", "wi_all", "ident", "causal"]


def kernel(**inputs):
    import concourse.bacc as bacc
    from concourse.bass_utils import run_bass_kernel_spmd

    arrays = _arrays({k: np.asarray(v) for k, v in inputs.items()})
    arrays = {k: np.ascontiguousarray(arrays[k]) for k in _ORDER}
    nc = bacc.Bacc("TRN2", target_bir_lowering=False, num_devices=1)
    args = [nc.dram_tensor(k, v.shape, mybir.dt.from_np(v.dtype), kind="ExternalInput").ap() for k, v in arrays.items()]
    out = nc.dram_tensor("out", (P, NT, W), mybir.dt.float32, kind="ExternalOutput").ap()
    block_kernel(nc, *args, out)
    res = run_bass_kernel_spmd(nc, [arrays], core_ids=[0]).results[0]["out"]
    return res.transpose(1, 0, 2).reshape(NB, T, W)
```

```python
import numpy as np
import concourse.bass as bass
from concourse import mybir
from contextlib import ExitStack

NB = 8
T = 256
W = 128
P = 128
H = 16
D = W // H
TOK = NB * T
NT = TOK // P
QT = T // P
HU = 512
HC = HU // P
STAGES = 9
INNER = 7
HS = 384
SC = HS // P
DEQUANT = float(np.float32(1.0 / 127.0))
QLORA, KVLORA, KVH = 64, 32, 4
PARTS = 3
SROWS = PARTS * PARTS * D
MROW = 96
VP = 32
QH = 4
HEADS = NB * H
QUADS = HEADS // QH
FT = 512
NF = TOK // FT
FS = FT // P
TILES = (NF, NB)
V_RING, E_RING = 2, 3
RING = 3
EPS = 1e-5
SCALE = float(D) ** -0.5
MASKED = -1e30
TWO_ONES = float(np.array([0x3F803F80], np.uint32).view(np.float32)[0])

LEAD, RAMP = 24, (23, 24)
AT_QK, AT_ROPE, AT_V = -48, -49, -4
AT_SPLIT = (-45, -43, -43, -40)
AT_OUT = -37
AT_IN = (-32, -28)
AT_MT = -6
PV_LAG = 8
MASK_LAG = 3
O_LAG = 12
AT_T, AT_ATT, AT_PROJ, AT_LN, AT_XT = (20, 22), 24, 29, 32, 35
FIRST = AT_QK
LATE, XB_AT, WF_AT = -1, 14, 27
BUTTERFLY, BF_STEP, WUP, JOIN = -6, 12, 92, 97
FIRST_BATCH = (-43, -45, -42, -42, -39, -39, -37, -33, -27)
LAST_BATCH = (20, 22, 25, 29, 31, 34)
HURRY = {(1, 0, step): at for step, at in zip((AT_QK, AT_ROPE, *AT_SPLIT, AT_OUT, *AT_IN), FIRST_BATCH)}
HURRY.update({(l, NB - 1, step): at for l in range(2)
              for step, at in zip((*AT_T, AT_ATT, AT_PROJ, AT_LN, AT_XT), LAST_BATCH)})
LAYER1 = dict(zip((AT_QK, AT_ROPE, AT_V, AT_MT, *AT_T, AT_ATT, AT_PROJ, AT_LN, AT_XT),
                  (-48, -46, -4, -6, 20, 22, 24, 29, 31, 34)))
SHIFT = 155
UP1 = (104, 107, 113, 117, 121, 126, 133, 155)
UP = ([[104, 104, 107, 107], [111, 111, 113, 113], [129, 131, 133, 135], [147, 148, 149, 150]],
      [[SHIFT + f + c for c in range(SC)] for f in UP1])
BACK = ([108, 115, 143, 153], [SHIFT + f + d for f, d in zip(UP1, (6, 8, 6, 6, 8, 5, 11, 3))])
F_LN, F_XT = 2, 4
SLOTS = range(FIRST, BACK[1][-1] + F_LN + 1)


def last_user(b, ring):
    return max(i for i in range(NB) if i % ring == b % ring)


def batch_at(l, g, offset):
    for b in range(NB):
        if g == H * b + HURRY.get((l, b, offset), LAYER1.get(offset, offset) if l == 1 else offset):
            return b
    return None


def maxima_at(l, g):
    def done(g):
        return max(0, min(HEADS, g + LEAD + 1, RAMP[l] + max(0, 5 * (g + 1) // 3)))
    return range(done(g - 1), done(g))


def at_slot(g, offset, every=H, count=NB):
    n, rest = divmod(g - offset, every)
    return n if rest == 0 and 0 <= n < count else None


def block_kernel(nc, x_nat, x_t, wqk0, wv0, bqk0, bv0, wproj, bproj, u0, d0, bfw, bup, bcon, bdown,
                 wqa_t, wqb, wkva_t, wkvb, wout, bout, rope_c, rope_s, wi_all, ident, causal, out):
    F32, BF, I32 = mybir.dt.float32, mybir.dt.bfloat16, mybir.dt.int32
    ALU = mybir.AluOpType
    ACT = mybir.ActivationFunctionType
    AX = mybir.AxisListType

    swap = nc.dram_tensor("butterfly_partners", [2, 2 * P * HC * (W + 1)], F32, kind="Internal").ap()
    scratch = nc.dram_tensor("qk_parts", [2, NB, 2, PARTS, P, T], BF, kind="Internal").ap()

    ctx = ExitStack()
    with ctx:
        def sb(name, shape, dt=F32):
            return ctx.enter_context(nc.sbuf_tensor(name, shape, dt))

        def sem(name):
            return ctx.enter_context(nc.semaphore(name))

        wqk_sb = sb("wqk_sb", [P, 2, W])
        wv_sb = sb("wv_sb", [P, W])
        bqk_sb = sb("bqk_sb", [P, 2])
        bv_sb = sb("bv_sb", [P, W])
        wproj_sb = sb("wproj_sb", [P, W])
        bproj_sb = sb("bproj_sb", [P, W])
        up = [sb(f"up{i}", [P, HC, W + 1]) for i in range(2)]
        down = [sb(f"down{i}", [P, HC, W]) for i in range(2)]
        own = sb("own", [P, 2, HC, W + 1])
        partner = sb("partner", [P, 2, HC, W + 1])
        bfw_sb = sb("bfw_sb", [P, 2, STAGES, 2, HC])
        bup_sb = sb("bup_sb", [P, HC])
        bhid = sb("bhid", [P, HC])
        bcon_sb = sb("bcon_sb", [P, W])
        bdown_sb = sb("bdown_sb", [P, W])
        wup = sb("wup", [P, HU])
        wqa_sb = sb("wqa_sb", [QLORA, W])
        wqb_sb = sb("wqb_sb", [QLORA, W])
        wkva_sb = sb("wkva_sb", [KVLORA, W])
        wkvb_sb = sb("wkvb_sb", [KVLORA, 2 * W])
        wl1 = sb("wl1", [P, 3, W])
        wout_sb = sb("wout_sb", [P, W])
        bout_sb = sb("bout_sb", [P, W])
        ropec_sb = sb("ropec_sb", [P, 2, T])
        ropes_sb = sb("ropes_sb", [P, 2, T])
        wi = sb("wi", [P, 3, HS], I32)
        wf = sb("wf", [P, 3, HS])
        id32 = sb("id32", [P, P])
        id16 = sb("id16", [P, P], BF)
        mask_sb = sb("mask_sb", [P, T])
        half = sb("half", [P, FS])
        xt = sb("xt", [P, TOK])
        xb = sb("xb", [P, NT, W])
        qk32 = sb("qk32", [P, 2, T])
        rope1 = sb("rope1", [P, 2, T])
        rope2 = sb("rope2", [P, 2, T])
        rest = sb("rest", [P, 2, T])
        parts = sb("parts", [P, 2, PARTS, 2, T], BF)
        Q = sb("Q", [P, 3, H, T], BF)
        K = sb("K", [P, 3, H, T], BF)
        V = sb("V", [P, V_RING, QT, H, VP])
        mx = sb("mx", [P, 2, QT, H])
        mrest = sb("mrest", [P, QT, H])
        mparts = sb("mparts", [P, QT, PARTS, H], BF)
        mt = sb("mt", [PARTS * H, 2, T], BF)
        E = sb("E", [P, E_RING, QH, 2 * T])
        O = sb("O", [P, 2, 2, 2, T])
        rec = sb("rec", [P, QT, H])
        at = sb("at", [P, QT, W])
        att = sb("att", [P, T])
        masked_s = sb("masked_s", [P, 2, T + P])
        NA, NFF = [{"r": sb(f"r_{k}", [P, n, W]), "stats": sb(f"stats_{k}", [P, n, 6]), "mv": sb(f"mv_{k}", [P, n, 2]),
                    "ve": sb(f"ve_{k}", [P, n]), "rstd": sb(f"rstd_{k}", [P, n]), "ln": sb(f"ln_{k}", [P, 2, n, W])}
                   for k, n in (("a", QT), ("f", FS))]
        hid = sb("hid", [P, 2, HC, FT])
        th = sb("th", [P, 2, T])
        gated = sb("gated", [P, 2, T])

        ST = [ctx.enter_context(nc.psum_tensor(f"ST{i}", [P, 512], F32)) for i in range(RING)]
        SM = [ctx.enter_context(nc.psum_tensor(f"SM{i}", [P, 512], F32)) for i in range(RING)]
        PV = ctx.enter_context(nc.psum_tensor("PV", [P, 512], F32))
        MISC = ctx.enter_context(nc.psum_tensor("MISC", [P, 512], F32))

        ld = {n: sem(f"ld_{n}") for n in ("qk", "x", "v", "id", "bf", "xb", "proj", "l1", "next", "rope", "gate")}
        q_clean, k_clean, v_clean = sem("q_clean"), sem("k_clean"), sem("v_clean")
        id16_ready = sem("id16_ready")
        partner_out, partner_in, stage_done = [[sem(f"{n}_{i}") for i in ("up", "down")]
                                               for n in ("partner_out", "partner_in", "stage_done")]
        wup_ps, wup_ready, bhid_ready = sem("wup_ps"), sem("wup_ready"), sem("bhid_ready")
        wl1_ps, wl1_ready, wf_ready = sem("wl1_ps"), sem("wl1_ready"), sem("wf_ready")
        xb0_ready, bnext_ready = sem("xb0_ready"), sem("bnext_ready")
        pool_chain, dve_chain = sem("pool_chain"), sem("dve_chain")
        AS = [{n: sem(f"a{l}_{n}") for n in (
            "qk_ps", "qk_out", "swapped", "rotated", "parts_ready", "wrote", "v_ps", "v_ready", "sm_ps", "max_done",
            "mparts_ready", "mt_ps", "mt_ready", "m_in", "st_ps", "exp_done", "masked", "pv_ps", "o_ready",
            "t_ps", "at_ready", "att_ps", "att_ready", "proj_ps", "res_done", "var_ready", "rstd_ready",
            "ln_ready", "xt_ps", "xt_ready", "xb_ready")} for l in range(2)]
        FF = [{n: sem(f"f{l}_{n}") for n in (
            "up_ps", "th_ready", "hid_ready", "down_ps", "res_done", "var_ready", "rstd_ready", "ln_ready",
            "xt_ps", "xt_ready", "xb_ready")} for l in range(2)]
        rows_in = [[[sem(f"a{l}_rows_in_{i}{h}") for h in range(2)] for i in range(2)] for l in range(2)]
        stored = [sem(f"stored{i}") for i in range(2)]

        def hidden0(n, c):
            return (SM if n < 2 else ST)[c % 2][:, :]

        def back0(n):
            return (SM if n < 2 else ST)[2]

        block = ctx.enter_context(nc.Block())

        def over_partitions(vec):
            return vec.rearrange("(a n) -> a n", a=1).broadcast_to([P, W])

        @block.sync
        def _(sp):
            sp.dma_start(xt[:, 0:T], x_t[:, 0:T]).then_inc(ld["x"], 16)
            sp.dma_start(wqk_sb[:, :, :], wqk0).then_inc(ld["qk"], 16)
            sp.dma_start(bqk_sb[:, :], bqk0).then_inc(ld["qk"], 16)
            sp.dma_start(xt[:, T:TOK], x_t[:, T:TOK]).then_inc(ld["x"], 16)
            sp.dma_start(wv_sb[:, :], wv0).then_inc(ld["v"], 16)
            sp.dma_start(bv_sb[:, :], over_partitions(bv0)).then_inc(ld["v"], 16)
            sp.dma_start(up[0][:, :, :], u0).then_inc(ld["bf"], 16)
            sp.dma_start(down[0][:, :, :], d0).then_inc(ld["bf"], 16)
            sp.dma_start(bfw_sb[:, :, :, :, :], bfw).then_inc(ld["bf"], 16)
            sp.dma_start(bup_sb[:, :], bup).then_inc(ld["bf"], 16)
            sp.dma_start(id32[:, :], ident).then_inc(ld["id"], 16)
            sp.dma_start(mask_sb[:, :], causal).then_inc(ld["id"], 16)

            late = [(ld["xb"], xb[:, :, :], x_nat), (ld["xb"], bproj_sb[:, :], over_partitions(bproj)),
                    (ld["proj"], wproj_sb[:, :], wproj)]
            late += [(ld["next"], dst[:, :], over_partitions(src))
                     for dst, src in ((bcon_sb, bcon), (bdown_sb, bdown), (bout_sb, bout))]
            late += [(ld["next"], wout_sb[:, :], wout)]
            late += [(ld["l1"], dst[:, :], src)
                     for dst, src in ((wqa_sb, wqa_t), (wqb_sb, wqb), (wkva_sb, wkva_t), (wkvb_sb, wkvb))]
            late += [(ld["rope"], ropec_sb[:, :, :], rope_c), (ld["rope"], ropes_sb[:, :, :], rope_s),
                     (ld["gate"], wi[:, :, :], wi_all)]

            def attention(l, g):
                S = AS[l]
                if (b := batch_at(l, g, AT_OUT)) is not None:
                    sp.wait_ge(S["parts_ready"], b + 1)
                    for s in range(2):
                        sp.dma_start(scratch[l, b, s].rearrange("a p t -> p a t"), parts[:, b % 2, :, s, :])\
                            .then_inc(S["wrote"], 16)
                for half_ in range(2):
                    if (b := batch_at(l, g, AT_IN[half_])) is not None:
                        if half_ == 0:
                            sp.wait_ge(S["wrote"], 32 * (b + 1))
                            if l == 0 and b < 3:
                                sp.wait_ge(q_clean, b + 1)
                                sp.wait_ge(k_clean, 2 * (b + 1))
                        if b >= 3:
                            sp.wait_ge(S["st_ps"], H * (b - 3) + H // 2 * (half_ + 1))
                        elif l == 1:
                            sp.wait_ge(AS[0]["st_ps"], H * (last_user(b, 3) + 1))
                        heads = slice(H // 2 * half_, H // 2 * (half_ + 1))
                        cols = slice(H // 2 * half_ * T, H // 2 * (half_ + 1) * T)
                        done = rows_in[l][b % 2][half_]
                        for a in range(PARTS):
                            sp.dma_start(Q[PARTS * D * a:PARTS * D * (a + 1), b % 3, heads, :],
                                         scratch[l, b, 0, a:a + 1].rearrange("a (d h) t -> a d (h t)", h=H)[:, :, cols]
                                         .broadcast_to([PARTS, D, H // 2 * T])).then_inc(done, 16)
                        sp.dma_start(K[0:SROWS, b % 3, heads, :],
                                     scratch[l, b, 1:2].rearrange("o a (d h) t -> o (a d) (h t)", h=H)[:, :, cols]
                                     .broadcast_to([PARTS, PARTS * D, H // 2 * T])).then_inc(done, 16)
                if (b := batch_at(l, g, AT_MT)) is not None:
                    sp.wait_ge(S["mt_ready"], b + 1)
                    for a in range(PARTS):
                        sp.dma_start(Q[MROW + a:MROW + a + 1, b % 3, :, :],
                                     mt[H * a:H * (a + 1), b % 2, :]).then_inc(S["m_in"], 16)

            def butterfly(g):
                for c, buf in enumerate((up, down)):
                    for k in range(STAGES):
                        stage = k if c == 0 else STAGES - 1 - k
                        at = BUTTERFLY + BF_STEP * k + BF_STEP // 2 * c
                        if stage >= INNER or g not in (at - 8, at - 4):
                            continue
                        swaps = k + 1 if c == 0 else INNER - stage
                        n = W + 1 if c == 0 else W
                        rows = swap[c, 0:2 * P * HC * n].rearrange("(m q s x) -> m q s x", q=4, s=1 << stage, x=HC * n)
                        if g == at - 8:
                            if k:
                                sp.wait_ge(stage_done[c], k)
                            else:
                                sp.wait_ge(ld["bf"], 64)
                            for j in range(2):
                                sp.dma_start(rows[:, 2 * j:2 * j + 2], buf[k % 2][:, :, 0:n]).then_inc(partner_out[c], 16)
                        else:
                            sp.wait_ge(partner_out[c], 32 * swaps)
                            sp.dma_start(partner[:, c, :, 0:n], rows[:, 1:3]).then_inc(partner_in[c], 16)

            for g in SLOTS:
                attention(0, g)
                if 0 <= g - LATE < len(late):
                    loaded, dst, src = late[g - LATE]
                    sp.dma_start(dst, src).then_inc(loaded, 16)
                butterfly(g)
                attention(1, g - SHIFT)
                for n in range(NB):
                    if g == BACK[1][n] + F_LN:
                        sp.wait_ge(FF[1]["ln_ready"], n + 1)
                        sp.dma_start(out[:, n * QT:(n + 1) * QT, :], NFF["ln"][:, n % 2, 0:QT, :]).then_inc(stored[n % 2], 16)
            for i in range(2):
                sp.wait_ge(stored[i], 16 * NB // 2)

        @block.tensor
        def _(pe):
            misc_read = []

            def misc(semaphore, value):
                if misc_read:
                    pe.wait_ge(*misc_read.pop())
                misc_read.append((semaphore, value))

            def turn_up():
                misc(wup_ready, 1)
                pe.wait_ge(stage_done[0], STAGES)
                pe.wait_ge(ld["id"], 32)
                for c in range(HC):
                    ins = nc.tensor.transpose(MISC[:, c * P:(c + 1) * P], up[1][:, c, 0:W], id32[:, :])
                ins.then_inc(wup_ps, 1)

            def join():
                misc(wl1_ready, 1)
                pe.wait_ge(ld["l1"], 64)
                nc.tensor.matmul(MISC[:, 0:W], wqa_sb[:, :], wqb_sb[:, :], start=True, stop=True)
                nc.tensor.matmul(MISC[:, W:3 * W], wkva_sb[:, :], wkvb_sb[:, :], start=True, stop=True).then_inc(wl1_ps, 1)

            def project(b, S, first, second):
                tokens = xt[:, b * T:(b + 1) * T]
                nc.tensor.matmul(MISC[:, 0:T], first, tokens, start=True, stop=True)
                nc.tensor.matmul(MISC[:, T:2 * T], second, tokens, start=True, stop=True).then_inc(S["qk_ps"], 1)

            def attention(l, g):
                S = AS[l]
                if (b := batch_at(l, g, AT_QK)) is not None:
                    misc(S["qk_out"], 2 * (b + 1) if l == 0 else b + 1)
                    if l == 0:
                        if b <= 1:
                            pe.wait_ge(ld["x"], 16 * (b + 1))
                        if b == 0:
                            pe.wait_ge(ld["qk"], 32)
                        project(b, S, wqk_sb[:, 0, :], wqk_sb[:, 1, :])
                    else:
                        if b % 2 == 0:
                            pe.wait_ge(FF[0]["xt_ready"], b // 2 + 1)
                        if b == 0:
                            pe.wait_ge(wl1_ready, 1)
                        project(b, S, wl1[:, 0, :], wl1[:, 1, :])
                if (b := batch_at(l, g, AT_V)) is not None:
                    misc(S["v_ready"], b + 1)
                    if l == 0 and b == 0:
                        pe.wait_ge(ld["v"], 32)
                    for k in range(QT):
                        ins = nc.tensor.matmul(MISC[:, k * P:(k + 1) * P], xt[:, b * T + k * P:b * T + (k + 1) * P],
                                               wv_sb[:, :] if l == 0 else wl1[:, 2, :], start=True, stop=True)
                    ins.then_inc(S["v_ps"], 1)
                if l == 0 and g == JOIN:
                    join()
                if l == 0 and g == WUP:
                    turn_up()
                for m in maxima_at(l, g):
                    b, h = divmod(m, H)
                    if h % (H // 2) == 0:
                        pe.wait_ge(rows_in[l][b % 2][h // (H // 2)], 64 * (b // 2 + 1))
                    if l == 1 and m == 0:
                        pe.wait_ge(FF[0]["xt_ready"], 2)
                    if m >= RING:
                        pe.wait_ge(S["max_done"], m - RING + 1)
                    bank = SM[m % RING]
                    if l == 0:
                        for q in range(QT):
                            ins = nc.tensor.matmul(bank[:, q * T:(q + 1) * T], Q[0:MROW, b % 3, h, q * P:(q + 1) * P],
                                                   K[0:MROW, b % 3, h, :], start=True, stop=True)
                    else:
                        nc.tensor.matmul(bank[:, 0:T], Q[0:MROW, b % 3, h, P:T], K[0:MROW, b % 3, h, :],
                                         start=True, stop=True)
                        ins = nc.tensor.matmul(bank[:, T:T + P], Q[0:MROW, b % 3, h, 0:P], K[0:MROW, b % 3, h, 0:P],
                                               start=True, stop=True)
                    ins.then_inc(S["sm_ps"], 1)
                if (b := batch_at(l, g, AT_MT)) is not None:
                    misc(S["mt_ready"], b + 1)
                    if l == 0 and b == 0:
                        pe.wait_ge(id16_ready, 1)
                    pe.wait_ge(S["mparts_ready"], b + 1)
                    for q in range(QT):
                        ins = nc.tensor.transpose(MISC[:, :].bitcast(BF)[0:PARTS * H, q * P:(q + 1) * P],
                                                  mparts[:, q, :, :], id16[:, :])
                    ins.then_inc(S["mt_ps"], 1)
                if 0 <= g < HEADS:
                    b, h = divmod(g, H)
                    if h == 0:
                        pe.wait_ge(S["m_in"], 48 * (b + 1))
                    if l == 1 and g == 0:
                        pe.wait_ge(FF[0]["hid_ready"], NF * HC)
                    if l == 1 and g == 2:
                        pe.wait_ge(FF[0]["xt_ready"], NF)
                    if g >= RING:
                        pe.wait_ge(S["exp_done"], g - RING + 1)
                    bank = ST[g % RING]
                    for k in range(QT):
                        q0 = k * P if l == 1 else 0
                        ins = nc.tensor.matmul(bank[:, k * T:(k + 1) * T - q0], K[:, b % 3, h, k * P:(k + 1) * P],
                                               Q[:, b % 3, h, q0:T], start=True, stop=True)
                    ins.then_inc(S["st_ps"], 1)
                if (a := at_slot(g, PV_LAG, QH, QUADS)) is not None:
                    b, r4 = divmod(a, H // QH)
                    if l == 0:
                        pe.wait_ge(S["exp_done"], QH * (a + 1))
                    else:
                        pe.wait_ge(S["masked"], 2 * (a + 1))
                    if r4 == 0:
                        pe.wait_ge(S["v_ready"], b + 1)
                    if a % 2 == 0 and a:
                        pe.wait_ge(S["o_ready"], a // 2)
                    elif l == 1 and a == 0:
                        pe.wait_ge(AS[0]["o_ready"], QUADS // 2)
                    for k in range(QT):
                        q0 = k * P if l == 1 else 0
                        for j in range(QH):
                            ins = nc.tensor.matmul(PV[VP * j:VP * (j + 1), a % 2 * T + q0:(a % 2 + 1) * T],
                                                   V[:, b % V_RING, k, QH * r4 + j, :], E[:, a % E_RING, j, k * T:(k + 1) * T - q0],
                                                   start=(k == 0), stop=(k == QT - 1))
                    ins.then_inc(S["pv_ps"], 1)
                for q in range(QT):
                    if (b := batch_at(l, g, AT_T[q])) is not None:
                        misc(S["at_ready"], QT * b + q + 1)
                        pe.wait_ge(S["o_ready"], 2 * (b + 1))
                        if l == 0 and b == 0:
                            pe.wait_ge(ld["id"], 32)
                        for a in range(H // QH):
                            ins = nc.tensor.transpose(MISC[:, a * P:(a + 1) * P],
                                                      O[:, b % 2, a // 2, a % 2, q * P:(q + 1) * P], id32[:, :])
                        ins.then_inc(S["t_ps"], 1)
                if (b := batch_at(l, g, AT_ATT)) is not None:
                    misc(S["att_ready"], b + 1)
                    pe.wait_ge(S["at_ready"], QT * (b + 1))
                    for q in range(QT):
                        ins = nc.tensor.transpose(MISC[:, q * P:(q + 1) * P], at[:, q, :], id32[:, :])
                    ins.then_inc(S["att_ps"], 1)
                if (b := batch_at(l, g, AT_PROJ)) is not None:
                    misc(S["res_done"], b + 1)
                    pe.wait_ge(S["att_ready"], b + 1)
                    if b == 0:
                        pe.wait_ge(ld["proj" if l == 0 else "next"], 16 if l == 0 else 64)
                    for q in range(QT):
                        ins = nc.tensor.matmul(MISC[:, q * P:(q + 1) * P], att[:, q * P:(q + 1) * P],
                                               (wproj_sb if l == 0 else wout_sb)[:, :], start=True, stop=True)
                    ins.then_inc(S["proj_ps"], 1)
                if (b := batch_at(l, g, AT_XT)) is not None:
                    misc(S["xt_ready"], b + 1)
                    pe.wait_ge(S["ln_ready"], b + 1)
                    for q in range(QT):
                        ins = nc.tensor.transpose(MISC[:, q * P:(q + 1) * P], NA["ln"][:, b % 2, q, :], id32[:, :])
                    ins.then_inc(S["xt_ps"], 1)

            def ffn(l, g):
                F = FF[l]
                C = HC if l == 0 else SC
                for n in range(TILES[l]):
                    for c in range(C):
                        if UP[l][n][c] != g:
                            continue
                        m = n * C + c
                        tokens = xt[:, n * TOK // TILES[l]:(n + 1) * TOK // TILES[l]]
                        if c == 0:
                            pe.wait_ge(AS[l]["xt_ready"], (n + 1) * NB // TILES[l])
                        if l == 0:
                            if m == 0:
                                pe.wait_ge(wup_ready, 1)
                                pe.wait_ge(AS[0]["max_done"], HEADS)
                            elif m == 2 * HC:
                                pe.wait_ge(AS[0]["exp_done"], HEADS)
                            if m % (2 * HC) >= 2:
                                pe.wait_ge(F["hid_ready"], m - 1)
                            nc.tensor.matmul(hidden0(n, c), wup[:, c * P:(c + 1) * P], tokens,
                                             start=True, stop=True).then_inc(F["up_ps"], 1)
                        else:
                            if m == 0:
                                pe.wait_ge(wf_ready, 2)
                                pe.wait_ge(AS[1]["max_done"], HEADS)
                            elif m >= 2:
                                pe.wait_ge(F["hid_ready"], m - 1)
                            for j in range(2):
                                ins = nc.tensor.matmul(SM[m % 2][:, j * T:(j + 1) * T], wf[:, j, c * P:(c + 1) * P], tokens,
                                                       start=True, stop=True)
                            ins.then_inc(F["up_ps"], 1)
                    if BACK[l][n] == g:
                        if l == 0:
                            if n % 2:
                                pe.wait_ge(F["xt_ready"], n)
                            if n == 0:
                                pe.wait_ge(stage_done[1], STAGES)
                        elif n:
                            pe.wait_ge(F["res_done"], n)
                        pe.wait_ge(F["hid_ready"], C * (n + 1))
                        bank = back0(n) if l == 0 else SM[2]
                        for s in range(FS * NF // TILES[l]):
                            for c in range(C):
                                w = down[1][:, c, :] if l == 0 else wf[:, 2, c * W:(c + 1) * W]
                                ins = nc.tensor.matmul(bank[:, s * W:(s + 1) * W], hid[:, n % 2, c, s * P:(s + 1) * P], w,
                                                       start=(c == 0), stop=(c == C - 1))
                        ins.then_inc(F["down_ps"], 1)
                    if l == 0 and BACK[l][n] + F_XT == g:
                        pe.wait_ge(F["res_done"], n + 1)
                        pe.wait_ge(F["ln_ready"], n + 1)
                        for s in range(FS):
                            ins = nc.tensor.transpose(back0(n)[:, s * P:(s + 1) * P], NFF["ln"][:, n % 2, s, :], id32[:, :])
                        ins.then_inc(F["xt_ps"], 1)

            for g in SLOTS:
                attention(0, g)
                ffn(0, g)
                attention(1, g - SHIFT)
                ffn(1, g)

        @block.scalar
        def _(act):
            def attention(l, g):
                S = AS[l]
                if l == 0 and (b := batch_at(l, g, AT_QK)) is not None:
                    if b == 0:
                        act.wait_ge(ld["qk"], 32)
                    else:
                        act.wait_ge(S["parts_ready"], b)
                    act.wait_ge(S["qk_ps"], b + 1)
                    for s in range(2):
                        act.activation(qk32[:, s, :], MISC[:, s * T:(s + 1) * T], ACT.Identity,
                                       bias=bqk_sb[:, s:s + 1]).then_inc(S["qk_out"], 1)
                if l == 1 and (b := batch_at(l, g, AT_QK)) is not None:
                    if b:
                        act.wait_ge(S["parts_ready"], b)
                    act.wait_ge(S["qk_ps"], b + 1)
                    act.activation(rope1[:, :, :], MISC[:, :].rearrange("p (s t) -> p s t", s=2), ACT.Copy)\
                        .then_inc(S["qk_out"], 1)
                    act.wait_ge(S["qk_out"], b + 1)
                    for lo in (0, P // 2):
                        hi = P // 2 - lo
                        act.activation(rope2[lo:lo + P // 2, :, :], rope1[hi:hi + P // 2, :, :], ACT.Copy)\
                            .then_inc(S["swapped"], 1)
                if l == 1 and (b := batch_at(l, g, AT_V)) is not None:
                    act.wait_ge(S["v_ps"], b + 1)
                    if b >= V_RING:
                        act.wait_ge(S["pv_ps"], H // QH * (b - V_RING + 1))
                    else:
                        act.wait_ge(AS[0]["pv_ps"], H // QH * (last_user(b, V_RING) + 1))
                    act.activation(V[:, b % V_RING, :, :, 0:D], MISC[:, 0:T].rearrange("p (k h d) -> p k h d", k=QT, h=H), ACT.Copy)\
                        .then_inc(S["v_ready"], 1)
                if l == 0 and g == WUP:
                    act.wait_ge(wup_ps, 1)
                    act.activation(wup[:, :], MISC[:, :], ACT.Copy).then_inc(wup_ready, 1)
                if l == 0 and g == JOIN:
                    act.wait_ge(wl1_ps, 1)
                    act.activation(wl1[:, :, :], MISC[:, 0:3 * W], ACT.Copy).then_inc(wl1_ready, 1)
                if (b := batch_at(l, g, AT_MT)) is not None:
                    act.wait_ge(S["mt_ps"], b + 1)
                    if b >= 2:
                        act.wait_ge(S["m_in"], 48 * (b - 1))
                    elif l == 1:
                        act.wait_ge(AS[0]["m_in"], 48 * NB)
                    act.activation(mt[:, b % 2, :], MISC[:, :].bitcast(BF)[0:PARTS * H, 0:T], ACT.Copy)\
                        .then_inc(S["mt_ready"], 1)
                if 0 <= g < HEADS:
                    a, j = divmod(g, QH)
                    act.wait_ge(S["st_ps"], g + 1)
                    if a >= E_RING:
                        act.wait_ge(S["pv_ps"], a - E_RING + 1)
                    elif l == 1:
                        act.wait_ge(AS[0]["pv_ps"], QUADS)
                    n = 2 * T if l == 0 else T + P
                    act.activation(E[:, a % E_RING, j, 0:n], ST[g % RING][:, 0:n], ACT.Exp, scale=SCALE)\
                        .then_inc(S["exp_done"], 1)
                if (n := at_slot(g, O_LAG, 2 * QH, QUADS // 2)) is not None:
                    b = n // 2
                    act.wait_ge(S["pv_ps"], 2 * (n + 1))
                    if b >= 2:
                        act.wait_ge(S["t_ps"], QT * (b - 1))
                    elif l == 1:
                        act.wait_ge(AS[0]["t_ps"], QT * NB)
                    act.activation(O[:, b % 2, n % 2, :, :], PV[:, :], ACT.Copy).then_inc(S["o_ready"], 1)
                if (b := batch_at(l, g, AT_ATT)) is not None:
                    act.wait_ge(S["att_ps"], b + 1)
                    if b:
                        act.wait_ge(S["proj_ps"], b)
                    elif l == 1:
                        act.wait_ge(AS[0]["proj_ps"], NB)
                    act.activation(att[:, :], MISC[:, 0:T], ACT.Copy).then_inc(S["att_ready"], 1)
                if (b := batch_at(l, g, AT_XT)) is not None:
                    act.wait_ge(S["xt_ps"], b + 1)
                    act.activation(xt[:, b * T:(b + 1) * T], MISC[:, 0:T], ACT.Copy).then_inc(S["xt_ready"], 1)

            def ffn(l, g):
                F = FF[l]
                C = HC if l == 0 else SC
                for n in range(TILES[l]):
                    for c in range(C):
                        if UP[l][n][c] != g:
                            continue
                        m = n * C + c
                        if l == 0:
                            if m == 0:
                                act.wait_ge(bhid_ready, 1)
                            if n >= 2:
                                act.wait_ge(F["down_ps"], n - 1)
                            act.wait_ge(F["up_ps"], m + 1)
                            act.activation(hid[:, n % 2, c, :], hidden0(n, c), ACT.Gelu, bias=bhid[:, c:c + 1])\
                                .then_inc(F["hid_ready"], 1)
                        else:
                            act.wait_ge(F["up_ps"], m + 1)
                            if m >= 2:
                                act.wait_ge(F["hid_ready"], m - 1)
                            act.activation(th[:, m % 2, :], SM[m % 2][:, 0:T], ACT.Tanh, scale=0.5).then_inc(F["th_ready"], 1)
                    if l == 0 and BACK[l][n] + F_XT == g:
                        act.wait_ge(F["xt_ps"], n + 1)
                        act.activation(xt[:, n * FT:(n + 1) * FT], back0(n)[:, :], ACT.Copy).then_inc(F["xt_ready"], 1)

            for g in SLOTS:
                attention(0, g)
                ffn(0, g)
                attention(1, g - SHIFT)
                ffn(1, g)

        @block.vector
        def _(dve):
            links = [0]

            def link(ins):
                links[0] += 1
                ins.then_inc(dve_chain, 1)
                dve.wait_ge(dve_chain, links[0])

            def split_first():
                p = parts[:, 0]
                dve.wait_ge(AS[0]["qk_out"], 2)
                link(nc.vector.tensor_copy(p[:, 0], qk32[:, :, :]))
                link(nc.vector.tensor_tensor(rest[:, :, :], qk32[:, :, :], p[:, 0], ALU.subtract))
                link(nc.vector.tensor_copy(p[:, 1], rest[:, :, :]))
                nc.vector.tensor_tensor(p[:, 2], rest[:, :, :], p[:, 1], ALU.subtract).then_inc(AS[0]["parts_ready"], 1)

            def clear_q(i):
                nc.vector.memset(Q[64:P, i, :, :].bitcast(F32), 0.0).then_inc(q_clean, 1)

            def statistics(N, n, var_ready):
                for s in range(n):
                    ins = nc.vector.bn_stats(N["stats"][:, s, :], N["r"][:, s, :])
                link(ins)
                for s in range(n):
                    ins = nc.vector.bn_aggr(N["mv"][:, s, :], N["stats"][:, s, :])
                link(ins)
                nc.vector.tensor_scalar(N["ve"][:, 0:n], N["mv"][:, 0:n, 1], EPS, None, ALU.add).then_inc(var_ready, 1)

            def normalise(N, n, parity, ln_ready):
                for s in range(n):
                    ins = nc.vector.tensor_scalar(N["ln"][:, parity, s, :], N["r"][:, s, :], N["mv"][:, s, 0:1],
                                                  N["rstd"][:, s:s + 1], ALU.subtract, ALU.mult)
                ins.then_inc(ln_ready, 1)

            def attention(l, g):
                S = AS[l]
                if l == 1 and (b := batch_at(l, g, AT_ROPE)) is not None:
                    if b == 0:
                        dve.wait_ge(ld["rope"], 32)
                    dve.wait_ge(S["swapped"], 2 * (b + 1))
                    for x, table in ((rope1, ropec_sb), (rope2, ropes_sb)):
                        nc.vector.tensor_tensor(x[:, :, :], x[:, :, :], table[:, :, :], ALU.mult).then_inc(S["rotated"], 1)
                if l == 0 and (b := batch_at(l, g, AT_V)) is not None:
                    dve.wait_ge(S["v_ps"], b + 1)
                    if b == 0:
                        dve.wait_ge(ld["v"], 32)
                        dve.wait_ge(v_clean, 2)
                    if b >= V_RING:
                        dve.wait_ge(S["pv_ps"], H // QH * (b - V_RING + 1))
                    values = V[:, b % V_RING, :, :, 0:D]
                    found = MISC[:, 0:T].rearrange("p (k h d) -> p k h d", k=QT, h=H)
                    for k in range(QT):
                        ins = nc.vector.tensor_tensor(values[:, k], found[:, k],
                                                      bv_sb[:, :].rearrange("p (h d) -> p h d", h=H), ALU.add)
                    ins.then_inc(S["v_ready"], 1)
                if l == 0 and g == AT_SPLIT[0]:
                    split_first()
                    clear_q(1)
                    nc.vector.memset(V[:, :, :, :, :], 0.0).then_inc(v_clean, 1)
                    dve.wait_ge(v_clean, 1)
                    nc.vector.memset(V[:, :, :, :, D:D + 1], 1.0).then_inc(v_clean, 1)
                    dve.wait_ge(ld["id"], 32)
                    nc.vector.tensor_copy(id16[:, :], id32[:, :]).then_inc(id16_ready, 1)
                    clear_q(2)
                for m in maxima_at(l, g):
                    b, h = divmod(m, H)
                    dve.wait_ge(S["sm_ps"], m + 1)
                    bank = SM[m % RING]
                    if l == 0:
                        ins = nc.vector.tensor_reduce(mx[:, b % 2, :, h], bank[:, :].rearrange("p (q k) -> p q k", q=QT),
                                                      AX.X, ALU.max, negate=True)
                    else:
                        if m >= 2:
                            dve.wait_ge(S["max_done"], m - 1)
                        for q, lo, hi in ((1, 0, T), (0, T, T + P)):
                            ins = nc.vector.tensor_tensor_reduce(
                                out=masked_s[:, m % 2, lo:hi], in0=bank[:, lo:hi], in1=mask_sb[:, T + lo - hi:T], scale=-1.0,
                                scalar=3.0e38, op0=ALU.add, op1=ALU.min, accum_out=mx[:, b % 2, q, h:h + 1])
                    ins.then_inc(S["max_done"], 1)
                    if h == H - 1:
                        dve.wait_ge(S["max_done"], m + 1)
                        if b:
                            dve.wait_ge(S["mt_ps"], b)
                        elif l == 1:
                            dve.wait_ge(AS[0]["mt_ps"], NB)
                        link(nc.vector.tensor_copy(mparts[:, :, 0, :], mx[:, b % 2, :, :]))
                        link(nc.vector.tensor_tensor(mrest[:, :, :], mx[:, b % 2, :, :], mparts[:, :, 0, :], ALU.subtract))
                        link(nc.vector.tensor_copy(mparts[:, :, 1, :], mrest[:, :, :]))
                        nc.vector.tensor_tensor(mparts[:, :, 2, :], mrest[:, :, :], mparts[:, :, 1, :], ALU.subtract)\
                            .then_inc(S["mparts_ready"], 1)
                for q in range(QT):
                    if (b := batch_at(l, g, AT_T[q])) is not None:
                        dve.wait_ge(S["t_ps"], QT * b + q + 1)
                        found = MISC[:, :].rearrange("p (h c) -> p h c", h=H)
                        link(nc.vector.reciprocal(rec[:, q, :], found[:, :, D]))
                        if b and q == 0:
                            dve.wait_ge(S["att_ps"], b)
                        elif l == 1 and b == 0:
                            dve.wait_ge(AS[0]["att_ps"], NB)
                        nc.vector.tensor_tensor(at[:, q, :].rearrange("p (h d) -> p h d", h=H), found[:, :, 0:D],
                                                rec[:, q, :].unsqueeze(2).broadcast_to([P, H, D]), ALU.mult)\
                            .then_inc(S["at_ready"], 1)
                if (b := batch_at(l, g, AT_PROJ)) is not None:
                    dve.wait_ge(S["proj_ps"], b + 1)
                    if l == 0 and b == 0:
                        dve.wait_ge(xb0_ready, 1)
                    if l == 1 and b % 2 == 0:
                        dve.wait_ge(FF[0]["xb_ready"], b // 2 + 1)
                    if b:
                        dve.wait_ge(S["ln_ready"], b)
                    elif l == 1:
                        dve.wait_ge(AS[0]["ln_ready"], NB)
                    nc.vector.tensor_tensor(NA["r"][:, :, :], MISC[:, 0:T].rearrange("p (q w) -> p q w", q=QT),
                                            xb[:, QT * b:QT * (b + 1), :], ALU.add).then_inc(S["res_done"], 1)
                    dve.wait_ge(S["res_done"], b + 1)
                    statistics(NA, QT, S["var_ready"])
                if (b := batch_at(l, g, AT_LN)) is not None:
                    dve.wait_ge(S["rstd_ready"], b + 1)
                    if b >= 2:
                        dve.wait_ge(S["xt_ps"], b - 1)
                        dve.wait_ge(S["xb_ready"], b - 1)
                    elif l == 1:
                        dve.wait_ge(AS[0]["xt_ps"], NB)
                        dve.wait_ge(AS[0]["xb_ready"], NB)
                    normalise(NA, QT, b % 2, S["ln_ready"])

            def ffn(l, g):
                F = FF[l]
                for n in range(TILES[l]):
                    for c in range(SC):
                        if l == 1 and UP[l][n][c] == g:
                            m = n * SC + c
                            if c == 0 and n >= 2:
                                dve.wait_ge(F["down_ps"], n - 1)
                            elif m == 0:
                                dve.wait_ge(FF[0]["down_ps"], NF)
                            dve.wait_ge(F["th_ready"], m + 1)
                            if m >= 2:
                                dve.wait_ge(F["hid_ready"], m - 1)
                            link(nc.vector.scalar_tensor_tensor(out=gated[:, m % 2, :], in0=th[:, m % 2, :], scalar=1.0,
                                                                in1=SM[m % 2][:, 0:T], op0=ALU.add, op1=ALU.mult))
                            nc.vector.tensor_tensor(hid[:, n % 2, c, 0:T], SM[m % 2][:, T:2 * T], gated[:, m % 2, :], ALU.mult)\
                                .then_inc(F["hid_ready"], 1)
                    if BACK[l][n] == g:
                        dve.wait_ge(F["down_ps"], n + 1)
                        dve.wait_ge(AS[l]["xb_ready"], (n + 1) * NB // TILES[l])
                        if n:
                            dve.wait_ge(F["ln_ready"], n)
                        elif l == 1:
                            dve.wait_ge(FF[0]["ln_ready"], NF)
                        bank = back0(n) if l == 0 else SM[2]
                        fs = NT // TILES[l]
                        nc.vector.tensor_tensor(NFF["r"][:, 0:fs, :], bank[:, 0:fs * W].rearrange("p (q w) -> p q w", q=fs),
                                                xb[:, fs * n:fs * (n + 1), :], ALU.add).then_inc(F["res_done"], 1)
                        dve.wait_ge(F["res_done"], n + 1)
                        statistics(NFF, fs, F["var_ready"])
                    if BACK[l][n] + F_LN == g:
                        dve.wait_ge(F["rstd_ready"], n + 1)
                        if l == 0 and n >= 2:
                            dve.wait_ge(F["xt_ps"], n - 1)
                            dve.wait_ge(F["xb_ready"], n - 1)
                        elif l == 1 and n < 2:
                            dve.wait_ge(FF[0]["xt_ps"], NF)
                            dve.wait_ge(FF[0]["xb_ready"], NF)
                        elif l == 1:
                            dve.wait_ge(stored[n % 2], 16 * (n // 2))
                        normalise(NFF, NT // TILES[l], n % 2, F["ln_ready"])

            clear_q(0)
            for g in SLOTS:
                attention(0, g)
                ffn(0, g)
                attention(1, g - SHIFT)
                ffn(1, g)

        @block.gpsimd
        def _(pool):
            links = [0]

            def link(ins):
                links[0] += 1
                ins.then_inc(pool_chain, 1)
                pool.wait_ge(pool_chain, links[0])

            def split(l, b, step):
                S = AS[l]
                p = parts[:, b % 2]
                if step == 0:
                    pool.wait_ge(S["qk_out" if l == 0 else "rotated"], 2 * (b + 1))
                    if l == 1:
                        if b:
                            pool.wait_ge(S["parts_ready"], b)
                        link(nc.gpsimd.tensor_tensor(qk32[:, :, :], rope1[:, :, :], rope2[:, :, :], ALU.add))
                elif step == 1:
                    if b >= 2:
                        pool.wait_ge(S["wrote"], 32 * (b - 1))
                    elif l == 1:
                        pool.wait_ge(AS[0]["wrote"], 32 * NB)
                    link(nc.gpsimd.tensor_scalar(p[:, 0], qk32[:, :, :], 1.0, 0.0, ALU.mult, ALU.add))
                    link(nc.gpsimd.tensor_tensor(rest[:, :, :], qk32[:, :, :], p[:, 0], ALU.subtract))
                elif step == 2:
                    link(nc.gpsimd.tensor_scalar(p[:, 1], rest[:, :, :], 1.0, 0.0, ALU.mult, ALU.add))
                else:
                    nc.gpsimd.tensor_tensor(p[:, 2], rest[:, :, :], p[:, 1], ALU.subtract).then_inc(S["parts_ready"], 1)

            def butterfly(k, c):
                buf, stage, n = (up, k, W + 1) if c == 0 else (down, STAGES - 1 - k, W)
                src, dst = buf[k % 2][:, :, 0:n], buf[(k + 1) % 2][:, :, 0:n]
                other = partner[:, c, :, 0:n]

                def weight(i, chunks=slice(0, HC)):
                    w = bfw_sb[:, c, stage, i, chunks].unsqueeze(2)
                    return w.broadcast_to([P, w.shape[1], n])

                if k == 0:
                    pool.wait_ge(ld["bf"], 64)
                else:
                    pool.wait_ge(stage_done[c], k)
                link(nc.gpsimd.tensor_tensor(own[:, c, :, 0:n], src, weight(0), ALU.mult))
                if stage < INNER:
                    pool.wait_ge(partner_in[c], 16 * (k + 1 if c == 0 else INNER - stage))
                    link(nc.gpsimd.tensor_tensor(other, other, weight(1), ALU.mult))
                else:
                    pairs = (slice(0, HC, 2), slice(1, HC, 2)) if stage == INNER else (slice(0, 2), slice(2, HC))
                    for here, there in (pairs, pairs[::-1]):
                        link(nc.gpsimd.tensor_tensor(other[:, here], src[:, there], weight(1, here), ALU.mult))
                nc.gpsimd.tensor_tensor(dst, own[:, c, :, 0:n], other, ALU.add).then_inc(stage_done[c], 1)

            def attention(l, g):
                S = AS[l]
                if l == 1 and (a := at_slot(g, MASK_LAG, QH, QUADS)) is not None:
                    pool.wait_ge(S["exp_done"], QH * (a + 1))
                    for c in (0, T):
                        e = E[:, a % E_RING, :, c:c + P]
                        nc.gpsimd.affine_select(out=e, in_=e, pattern=[[0, QH], [1, P]], compare_op=ALU.is_ge,
                                                fill=0.0, base=0, channel_multiplier=-1).then_inc(S["masked"], 1)
                for step in range(len(AT_SPLIT)):
                    if (b := batch_at(l, g, AT_SPLIT[step])) is not None and (l, b) != (0, 0):
                        split(l, b, step)
                if l == 0 and g == H + AT_SPLIT[-1] + 1:
                    pool.wait_ge(S["parts_ready"], 2)
                    clear(2)
                if l == 0:
                    for c in range(2):
                        if (k := at_slot(g, BUTTERFLY + BF_STEP // 2 * c, BF_STEP, STAGES)) is not None:
                            butterfly(k, c)
                if l == 0 and g == WUP:
                    pool.wait_ge(stage_done[0], STAGES)
                    nc.gpsimd.tensor_tensor(bhid[:, :], up[1][:, :, W], bup_sb[:, :], ALU.add).then_inc(bhid_ready, 1)
                if l == 0 and g == XB_AT:
                    pool.wait_ge(ld["xb"], 32)
                    nc.gpsimd.tensor_tensor(xb[:, :, :], xb[:, :, :],
                                            bproj_sb[:, :].unsqueeze(1).broadcast_to([P, NT, W]), ALU.add)\
                        .then_inc(xb0_ready, 1)
                    pool.wait_ge(ld["next"], 64)
                    nc.gpsimd.tensor_tensor(bcon_sb[:, :], bcon_sb[:, :], bdown_sb[:, :], ALU.add)\
                        .then_inc(bnext_ready, 1)
                if l == 0 and g == WF_AT:
                    pool.wait_ge(ld["gate"], 16)
                    for j, scale in ((slice(0, 2), 1.0), (slice(2, 3), 0.5)):
                        nc.gpsimd.tensor_scalar(wf[:, j, :], wi[:, j, :], scale * DEQUANT, 0.0, ALU.mult, ALU.add)\
                            .then_inc(wf_ready, 1)
                if (b := batch_at(l, g, AT_PROJ)) is not None:
                    pool.wait_ge(S["var_ready"], b + 1)
                    nc.gpsimd.tensor_tensor(NA["rstd"][:, :], NA["ve"][:, :], half[:, 0:QT], ALU.pow).then_inc(S["rstd_ready"], 1)
                if (b := batch_at(l, g, AT_LN)) is not None:
                    pool.wait_ge(S["ln_ready"], b + 1)
                    dst, src = xb[:, QT * b:QT * (b + 1), :], NA["ln"][:, b % 2, :, :]
                    if l == 0:
                        if b == 0:
                            pool.wait_ge(bnext_ready, 1)
                        nc.gpsimd.tensor_tensor(dst, src, bcon_sb[:, :].unsqueeze(1).broadcast_to([P, QT, W]), ALU.add)\
                            .then_inc(S["xb_ready"], 1)
                    else:
                        nc.gpsimd.tensor_scalar(dst, src, 1.0, 0.0, ALU.mult, ALU.add).then_inc(S["xb_ready"], 1)

            def ffn(l, g):
                F = FF[l]
                for n in range(TILES[l]):
                    if BACK[l][n] == g:
                        pool.wait_ge(F["var_ready"], n + 1)
                        fs = NT // TILES[l]
                        nc.gpsimd.tensor_tensor(NFF["rstd"][:, 0:fs], NFF["ve"][:, 0:fs], half[:, 0:fs], ALU.pow)\
                            .then_inc(F["rstd_ready"], 1)
                    if l == 0 and BACK[l][n] + F_LN == g:
                        pool.wait_ge(F["ln_ready"], n + 1)
                        nc.gpsimd.tensor_tensor(xb[:, FS * n:FS * (n + 1), :], NFF["ln"][:, n % 2, :, :],
                                                bout_sb[:, :].unsqueeze(1).broadcast_to([P, FS, W]), ALU.add)\
                            .then_inc(F["xb_ready"], 1)

            def clear(i):
                nc.gpsimd.memset(K[64:P, i, :, :].bitcast(F32), 0.0).then_inc(k_clean, 1)
                pool.wait_ge(k_clean, 2 * i + 1)
                nc.gpsimd.memset(K[MROW:MROW + PARTS, i, :, :].bitcast(F32), TWO_ONES).then_inc(k_clean, 1)
                pool.wait_ge(k_clean, 2 * i + 2)

            link(nc.gpsimd.memset(half[:, :], -0.5))
            for i in range(2):
                clear(i)
            for g in SLOTS:
                attention(0, g)
                ffn(0, g)
                attention(1, g - SHIFT)
                ffn(1, g)


def _features():
    d, h = np.meshgrid(np.concatenate([np.arange(0, D, 2), np.arange(1, D, 2)]), np.arange(H), indexing="ij")
    return d.ravel(), h.ravel()


def _constants():
    d, _ = _features()
    inv = (1.0 / np.float32(10000.0) ** (np.arange(0, D, 2, dtype=np.float32) / np.float32(D))).astype(np.float32)
    freqs = np.outer(np.arange(T, dtype=np.float32), inv).astype(np.float32)
    c = np.cos(freqs).astype(np.float32).T[d // 2]
    s = np.sin(freqs).astype(np.float32).T[d // 2] * np.where(d % 2 == 0, -1.0, 1.0).astype(np.float32)[:, None]
    i = np.arange(P)
    later = np.where(i[None, :] > i[:, None], np.float32(MASKED), np.float32(0.0))
    return {
        "rope_c": np.stack([c, c], 1), "rope_s": np.stack([s, s], 1),
        "ident": np.eye(P, dtype=np.float32), "causal": np.concatenate([later, later], 1).astype(np.float32),
    }


def _butterfly_layout(up_weights, down_weights):
    f = np.arange(HU)
    out = np.empty((HU, 2, STAGES, 2), np.float32)
    for s in range(STAGES):
        k, j = (f >> (s + 1) << s) + f % (1 << s), f >> s & 1
        out[:, 0, s, 0], out[:, 0, s, 1] = up_weights[s, k, j, j], up_weights[s, k, j, 1 - j]
        out[:, 1, s, 0], out[:, 1, s, 1] = down_weights[s, k, j, j], down_weights[s, k, 1 - j, j]
    return out.reshape(HC, P, 2, STAGES, 2).transpose(1, 2, 3, 4, 0)


def _arrays(a):
    d, h = _features()
    wqkv, bqkv = a["L0_attn_Wqkv"], a["L0_attn_bqkv"]
    x = a["L0_attn_x"].reshape(NT, P, W)
    heads, dims = np.arange(W) // D, np.arange(W) % D
    cols = [3 * D * h + d, 3 * D * h + D + d, 3 * D * heads + 2 * D + dims]
    rep = H // KVH
    kcol = [2 * D * (h // rep) + 2 * d, 2 * D * (heads // rep) + 2 * dims + 1]
    u = np.concatenate([a["L0_ffn_W_exp"].T, a["L0_ffn_b_exp"][:, None]], 1)
    out = {
        "x_nat": x.transpose(1, 0, 2), "x_t": x.reshape(TOK, W).T,
        "wqk0": np.stack([wqkv[:, cols[0]], wqkv[:, cols[1]]], 1), "wv0": wqkv[:, cols[2]],
        "bqk0": np.stack([bqkv[cols[0]], bqkv[cols[1]]], 1), "bv0": bqkv[cols[2]],
        "wproj": a["L0_attn_Wproj"], "bproj": a["L0_attn_bproj"],
        "u0": u.reshape(HC, P, W + 1).transpose(1, 0, 2),
        "d0": a["L0_ffn_W_con"].reshape(HC, P, W).transpose(1, 0, 2),
        "bfw": _butterfly_layout(a["L0_ffn_up_weights"], a["L0_ffn_down_weights"]),
        "bup": a["L0_ffn_up_bias"].reshape(HC, P).T,
        "bcon": a["L0_ffn_b_con"], "bdown": a["L0_ffn_down_bias"],
        "wqa_t": a["L1_attn_Wqa"].T,
        "wqb": a["L1_attn_Wqb"][:, D * h + d],
        "wkva_t": a["L1_attn_Wkva"].T,
        "wkvb": np.concatenate([a["L1_attn_Wkvb"][:, c] for c in kcol], 1),
        "wout": a["L1_attn_Wout"], "bout": a["L1_attn_bout"],
        "wi_all": np.stack([a["L1_ffn_w_gate"].T, a["L1_ffn_w_up"].T,
                            a["L1_ffn_w_down"].T.reshape(SC, P, W).transpose(1, 0, 2).reshape(P, HS)], 1),
    }
    out.update(_constants())
    return out


_ORDER = ["x_nat", "x_t", "wqk0", "wv0", "bqk0", "bv0", "wproj", "bproj", "u0", "d0", "bfw", "bup", "bcon", "bdown",
          "wqa_t", "wqb", "wkva_t", "wkvb", "wout", "bout", "rope_c", "rope_s", "wi_all", "ident", "causal"]


def kernel(**inputs):
    import concourse.bacc as bacc
    from concourse.bass_utils import run_bass_kernel_spmd

    arrays = _arrays({k: np.asarray(v) for k, v in inputs.items()})
    arrays = {k: np.ascontiguousarray(arrays[k]) for k in _ORDER}
    nc = bacc.Bacc("TRN2", target_bir_lowering=False, num_devices=1)
    args = [nc.dram_tensor(k, v.shape, mybir.dt.from_np(v.dtype), kind="ExternalInput").ap() for k, v in arrays.items()]
    out = nc.dram_tensor("out", (P, NT, W), mybir.dt.float32, kind="ExternalOutput").ap()
    block_kernel(nc, *args, out)
    res = run_bass_kernel_spmd(nc, [arrays], core_ids=[0]).results[0]["out"]
    return res.transpose(1, 0, 2).reshape(NB, T, W)
```
